# Optimizing a Trainium2 kernel written in Bass

```python
import numpy as np
import jax
import jax.numpy as jnp

def _softmax(x, axis=-1):
    return jax.nn.softmax(x, axis=axis)

def _gelu(x):
    return jax.nn.gelu(x, approximate=True)

def _silu(x):
    return jax.nn.silu(x)

def _sigmoid(x):
    return jax.nn.sigmoid(x)

def _layernorm(x, axis=-1, eps=1e-05):
    m = jnp.mean(x, axis=axis, keepdims=True)
    v = jnp.var(x, axis=axis, keepdims=True)
    return (x - m) / jnp.sqrt(v + eps)

def _scatter_add(tgt, idx, src, axis=0):
    return tgt.at[idx].add(src)

def _segment_sum(src, seg, n):
    return jax.ops.segment_sum(src, seg, n)
kernel_name = 'mk_xattn_ffn_d1_seqx_r4_cef4a8'

def setup_inputs(seed: int=0):
    np.random.seed(seed)
    _w = jnp.asarray

    def _rec_inputs():
        import jax
        import jax.numpy as jnp
        _rk = jax.random.key(seed)
        x = 7.22e-05 + 1 * jax.random.normal(jax.random.fold_in(_rk, 1), (16, 256, 512), jnp.float32)
        _lenS = 256 - jax.random.randint(jax.random.fold_in(_rk, 7), (16,), 0, max(1, 256 // 4) + 1, jnp.int32)
        _lenS2 = 256 - jax.random.randint(jax.random.fold_in(_rk, 8), (16,), 0, max(1, 256 // 4) + 1, jnp.int32)
        _ctx_2048P = jax.random.normal(jax.random.fold_in(_rk, 11), (16, 16, 512), jnp.float32)
        _ctx_2048c = jax.random.dirichlet(jax.random.fold_in(_rk, 511), 0.3 * jnp.ones((16,), jnp.float32), (16, 256))
        _ctx_2048t = jnp.einsum('bsk,bkd->bsd', _ctx_2048c, _ctx_2048P)
        _ctx_2048t = _ctx_2048t * jax.lax.rsqrt(jnp.mean(jnp.square(_ctx_2048t)) + 1e-12) * 0.953939
        ctx_2048 = 4.13588e-05 + 0.999923 * (_ctx_2048t + 0.3 * jax.random.normal(jax.random.fold_in(_rk, 611), (16, 256, 512), jnp.float32))
        return (x, ctx_2048)
    x, ctx_2048 = _rec_inputs()

    def _L0_xattn_setup():
        import jax, jax.numpy as jnp
        import numpy as np
        N_HEADS = 16
        K_CH = 256 // N_HEADS
        SCALE = 1.0 / np.sqrt(K_CH)
        key = jax.random.key(seed)
        ks = jax.random.split(key, 10)
        B, C, T = (4, 256, 512)
        Cout = 256
        xavier = lambda k, o, i: jax.random.uniform(k, (o, i), jnp.float32, -1.0, 1.0) * np.sqrt(6.0 / (o + i))
        return {'x': jax.random.normal(ks[0], (B, C, T), jnp.float32), 'c': jax.random.normal(ks[1], (B, C, T), jnp.float32), 'Wq': xavier(ks[2], C, C), 'bq': jnp.zeros((C,), jnp.float32), 'Wk': xavier(ks[3], C, C), 'bk': jnp.zeros((C,), jnp.float32), 'Wv': xavier(ks[4], C, C), 'bv': jnp.zeros((C,), jnp.float32), 'Wo': xavier(ks[5], Cout, C), 'bo': jnp.zeros((Cout,), jnp.float32)}
    _L0_xattn_all = _L0_xattn_setup()
    _L0_xattn_in = {k: v for k, v in _L0_xattn_all.items() if k in ('Wq', 'bq', 'Wk', 'bk', 'Wv', 'bv', 'Wo', 'bo')}
    del _L0_xattn_all

    def _L0_ffn_setup():
        import jax, jax.numpy as jnp
        import numpy as np
        RANK = 64
        SCALING = 1.0 / RANK
        TEMPERATURE = 1.0
        key = jax.random.key(seed)
        k_x, k_a, k_b, k_w = jax.random.split(key, 4)
        B_, S, D = (4, 512, 512)
        E, R, O = (8, RANK, 512)
        x = jax.random.normal(k_x, (B_, S, D), dtype=jnp.float32)
        A = jax.random.normal(k_a, (E, R, D), dtype=jnp.float32) * (1.0 / np.sqrt(D))
        Bw = jax.random.normal(k_b, (E, O, R), dtype=jnp.float32) * 0.02
        Wr = jax.random.normal(k_w, (E, D), dtype=jnp.float32) * (1.0 / np.sqrt(D))
        br = jnp.zeros((E,), dtype=jnp.float32)
        return {'x': x, 'A': A, 'B': Bw, 'Wr': Wr, 'br': br}
    _L0_ffn_all = _L0_ffn_setup()
    _L0_ffn_in = {k: v for k, v in _L0_ffn_all.items() if k in ('A', 'B', 'Wr', 'br')}
    del _L0_ffn_all
    return {'x': x, 'ctx_2048': ctx_2048, 'L0_xattn_Wq': _L0_xattn_in['Wq'], 'L0_xattn_bq': _L0_xattn_in['bq'], 'L0_xattn_Wk': _L0_xattn_in['Wk'], 'L0_xattn_bk': _L0_xattn_in['bk'], 'L0_xattn_Wv': _L0_xattn_in['Wv'], 'L0_xattn_bv': _L0_xattn_in['bv'], 'L0_xattn_Wo': _L0_xattn_in['Wo'], 'L0_xattn_bo': _L0_xattn_in['bo'], 'L0_ffn_A': _L0_ffn_in['A'], 'L0_ffn_B': _L0_ffn_in['B'], 'L0_ffn_Wr': _L0_ffn_in['Wr'], 'L0_ffn_br': _L0_ffn_in['br']}

def reference(x, ctx_2048, L0_xattn_Wq, L0_xattn_bq, L0_xattn_Wk, L0_xattn_bk, L0_xattn_Wv, L0_xattn_bv, L0_xattn_Wo, L0_xattn_bo, L0_ffn_A, L0_ffn_B, L0_ffn_Wr, L0_ffn_br):
    import jax
    import jax.numpy as jnp

    def _L0_xattn_ref(x, c, Wq, bq, Wk, bk, Wv, bv, Wo, bo):
        import jax, jax.numpy as jnp
        import numpy as np
        N_HEADS = 16
        K_CH = 256 // N_HEADS
        SCALE = 1.0 / np.sqrt(K_CH)
        B, C, T = x.shape
        H, K = (N_HEADS, K_CH)
        q = jnp.einsum('oc,bct->bot', Wq, x) + bq[None, :, None]
        k = jnp.einsum('oc,bct->bot', Wk, c) + bk[None, :, None]
        v = jnp.einsum('oc,bct->bot', Wv, c) + bv[None, :, None]
        q = q.reshape(B, H, K, T)
        k = k.reshape(B, H, K, -1)
        v = v.reshape(B, H, K, -1)
        scores = jnp.einsum('bhkt,bhks->bhts', q, k) * SCALE
        p = jax.nn.softmax(scores, axis=-1)
        out = jnp.einsum('bhts,bhks->bhkt', p, v)
        out = out.reshape(B, H * K, T)
        return jnp.einsum('oc,bct->bot', Wo, out) + bo[None, :, None]

    def _L0_ffn_ref(x, A, B, Wr, br):
        import jax, jax.numpy as jnp
        import numpy as np
        RANK = 64
        SCALING = 1.0 / RANK
        TEMPERATURE = 1.0
        batch, seq, d = x.shape
        E, out_dim = (B.shape[0], B.shape[1])
        x_flat = x.reshape(-1, d)
        logits = (x_flat @ Wr.T + br) / TEMPERATURE
        probs = jax.nn.softmax(logits, axis=-1)
        expert_idx = jnp.argmax(probs, axis=-1)
        expert_weight = jnp.max(probs, axis=-1)
        h = jnp.einsum('nd,erd->ner', x_flat, A)
        y = jnp.einsum('ner,eor->neo', h, B) * SCALING
        sel = jnp.take_along_axis(y, expert_idx[:, None, None], axis=1)[:, 0, :]
        out_flat = sel * expert_weight[:, None]
        return out_flat.reshape(batch, seq, out_dim)
    x = x + _L0_xattn_ref(_layernorm(x, axis=-1), ctx_2048, L0_xattn_Wq, L0_xattn_bq, L0_xattn_Wk, L0_xattn_bk, L0_xattn_Wv, L0_xattn_bv, L0_xattn_Wo, L0_xattn_bo)
    x = x + _L0_ffn_ref(_layernorm(x, axis=-1), L0_ffn_A, L0_ffn_B, L0_ffn_Wr, L0_ffn_br)
    return x

_drawn_inputs = setup_inputs


def setup_inputs(seed=0):
    import zlib

    import numpy as np

    out = dict(_drawn_inputs(seed))
    spreads = {'L0_xattn_bq': (0.0, 0.1),
     'L0_xattn_bk': (0.0, 0.8),
     'L0_xattn_bv': (0.0, 0.1),
     'L0_xattn_bo': (0.0, 0.1),
     'L0_ffn_br': (0.0, 0.8)}
    factors = {'L0_ffn_A': 8.0, 'L0_ffn_B': 8.0, 'L0_ffn_Wr': 8.0}
    for name, (base, spread) in spreads.items():
        noise = np.random.default_rng([zlib.crc32(name.encode()), seed]).standard_normal(out[name].shape)
        drawn = base * np.exp(spread * noise) if base else spread * noise
        out[name] = jnp.asarray(drawn.astype(out[name].dtype))
    for name, factor in factors.items():
        out[name] = (out[name] * factor).astype(out[name].dtype)
    return out
```

```python
from contextlib import ExitStack

import concourse.bass as bass
from concourse import mybir

F32 = mybir.dt.float32
F32R = mybir.dt.float32r
ALU = mybir.AluOpType
ACT = mybir.ActivationFunctionType
X_AXIS = mybir.AxisListType.X

P = 128
BATCHES, C, T = 16, 256, 512
HEADS, KC = 16, 16
SCALE = float(KC) ** -0.5
E, R, D = 8, 64, 512
EPS = 1e-5

CH = C // P
DCH = D // P
QUADS = HEADS // 4
PIECES = T // P
STEPS = QUADS * PIECES
LAG = STEPS // 2
UNITS = 4 * STEPS
SPLIT_ROWS = 96
FULL_ROWS = SPLIT_ROWS + 2
NORM = 14
QUAD_NORM = [0, 3, 7, 10]
ROUTE = 10
BLOCKS = T // 32

SIDE_WORK = [
    ("logit_turn", -2, 0), ("hidden0", -2, 1), ("max3", -1, 0), ("hidden1", -2, 1), ("hidden_turn0", -2, 0),
    ("q0", 1, 1), ("max0", 0, 0), ("k0", 1, 1), ("hidden_turn1", -2, 0), ("y0", -2, 1), ("y1", -2, 0),
    ("max1", 0, 1), ("v0", 1, 0), ("out0", -1, 1), ("out1", -1, 0), ("q1", 1, 1), ("max2", 0, 0),
    ("k1", 1, 1), ("v1", 1, 0), ("x_turn0", -1, 1), ("x_turn1", -1, 0), ("logits", -1, 1),
]
FIRST_FULL, LAST_FULL = 3, BATCHES - 3


class Iteration:

    def __init__(self, b, looped=False):
        self.b, self.looped = b, looped

    def live(self, offset):
        return self.looped or 0 <= self.b + offset < BATCHES


def counts(n):
    return not isinstance(n, int) or n > 0


def stand_alone(eng, sem):
    eng.sem_inc(sem, 1)


def run_iterations(eng, body):
    for b in range(-1, FIRST_FULL):
        body(Iteration(b))
    with eng.Fori(FIRST_FULL, LAST_FULL + 1) as b:
        body(Iteration(b, looped=True))
    for b in range(LAST_FULL + 1, BATCHES + 2):
        body(Iteration(b))


def xattn_experts(nc, x, ctx_in, wq_t, wk_t, wv_t, wo_t, bq, bk, bv, bo, a_t, b_t, wr_t, br, out):
    with ExitStack() as stack:
        def sb(name, shape, dt=F32):
            return stack.enter_context(nc.sbuf_tensor(name, shape, dt))

        def bank(name):
            return stack.enter_context(nc.psum_tensor(name, [P, 512], F32))

        def sem(name):
            return stack.enter_context(nc.semaphore(name))

        wq_sb = sb("wq_sb", [P, CH, C])
        wk_sb = sb("wk_sb", [P, CH, C])
        wv_sb = sb("wv_sb", [P, CH, C])
        wo_sb = sb("wo_sb", [P, CH, C])
        bq_sb = sb("bq_sb", [P, CH])
        bk_sb = sb("bk_sb", [P, CH])
        bv_sb = sb("bv_sb", [P, C])
        bo_sb = sb("bo_sb", [P, CH])
        a_sb = sb("a_sb", [P, DCH, E * R])
        b_sb = sb("b_sb", [P, DCH, D])
        wr_sb = sb("wr_sb", [P, DCH, E])
        br_sb = sb("br_sb", [E, 1])
        ident = sb("ident", [P, P])
        rank = sb("rank", [P, CH, E])
        minus_half = sb("minus_half", [P, CH])

        x_raw = sb("x_raw", [P, CH, T])
        ctx_sb = sb("ctx_sb", [P, CH, T])
        xn = sb("xn", [P, CH, T])
        q_hi = sb("q_hi", [P, CH, T], F32R)
        q_lo = sb("q_lo", [P, CH, T], F32R)
        k_hi = sb("k_hi", [P, CH, T], F32R)
        k_lo = sb("k_lo", [P, CH, T], F32R)
        q_stack = sb("q_stack", [P, HEADS, T], F32R)
        k_stack = sb("k_stack", [P, HEADS, T], F32R)
        neg_max = sb("neg_max", [P, QUADS, PIECES, 4])
        max_rows = sb("max_rows", [4, 2, T], F32R)
        probs = sb("probs", [P, 2, 4, T])
        v_plain = sb("v_plain", [P, PIECES, C])
        v_ones = sb("v_ones", [P, QUADS, PIECES, 4, 32])
        turned = sb("turned", [P, BLOCKS, 32])
        inv_sum = sb("inv_sum", [P, BLOCKS, 1])
        normed = sb("normed", [P, BLOCKS, 32])
        heads_out = sb("heads_out", [P, CH, T])

        x_again = sb("x_again", [P, CH, T])
        x2 = sb("x2", [P, CH, T])
        xn2 = sb("xn2", [P, CH, T])
        xn2_t = sb("xn2_t", [P, CH, DCH, P])
        stats1 = sb("stats1", [P, CH, 6])
        mean_var1 = sb("mean_var1", [P, CH, 2])
        var_eps1 = sb("var_eps1", [P, CH])
        rstd1 = sb("rstd1", [P, CH])
        stats2 = sb("stats2", [P, CH, 6])
        mean_var2 = sb("mean_var2", [P, CH, 2])
        var_eps2 = sb("var_eps2", [P, CH])
        rstd2 = sb("rstd2", [P, CH])
        logits_t = sb("logits_t", [E, CH * P])
        logit = sb("logit", [P, CH, E])
        top = sb("top", [P, CH, 1])
        below_top = sb("below_top", [P, CH, E])
        exp_logit = sb("exp_logit", [P, CH, E])
        exp_sum = sb("exp_sum", [P, CH, 1])
        weight = sb("weight", [P, CH, 1])
        is_top = sb("is_top", [P, CH, E])
        top_rank = sb("top_rank", [P, CH, E])
        best_rank = sb("best_rank", [P, CH, 1])
        chosen = sb("chosen", [P, CH, E])
        gate = sb("gate", [P, CH, E])
        hidden = sb("hidden", [P, CH, E * R])
        hidden_t = sb("hidden_t", [P, CH, DCH, P])
        y_out = sb("y_out", [P, CH, D])

        s1_bank = [bank(f"s1_bank{i}") for i in range(2)]
        s2_bank = [bank(f"s2_bank{i}") for i in range(2)]
        pv_bank = [bank(f"pv_bank{i}") for i in range(2)]
        side_bank = [bank(f"side_bank{i}") for i in range(2)]
        bank_of = {name: side_bank[k] for name, _, k in SIDE_WORK}

        weights_in = sem("weights_in")
        ones_set = sem("ones_set")
        pad_set = sem("pad_set")
        ident_set = sem("ident_set")
        passed = sem("passed")
        x_in = sem("x_in")
        ctx_in_sem = sem("ctx_in_sem")
        x_again_in = sem("x_again_in")
        stack_in = [sem(f"stack_in{q}") for q in range(QUADS)]
        max_rows_in = [sem(f"max_rows_in{q}") for q in range(QUADS)]
        out_stored = [sem(f"out_stored{t}") for t in range(CH)]
        s1_ready = sem("s1_ready")
        max_done = sem("max_done")
        s2_ready = sem("s2_ready")
        exp_done = sem("exp_done")
        pv_done = sem("pv_done")
        norm_done = sem("norm_done")
        qk_ready = sem("qk_ready")
        qk_hi_done = sem("qk_hi_done")
        qk_lo_done = sem("qk_lo_done")
        v_ready = sem("v_ready")
        v_plain_done = sem("v_plain_done")
        v_ones_done = sem("v_ones_done")
        max_turned = sem("max_turned")
        max_hi_done = sem("max_hi_done")
        max_lo_done = sem("max_lo_done")
        out_ready = sem("out_ready")
        x2_done = sem("x2_done")
        x_turned = sem("x_turned")
        xn2_t_done = sem("xn2_t_done")
        logits_ready = sem("logits_ready")
        logits_t_done = sem("logits_t_done")
        logit_turned = sem("logit_turned")
        hidden_ready = sem("hidden_ready")
        hidden_done = sem("hidden_done")
        hidden_turned = sem("hidden_turned")
        hidden_t_done = sem("hidden_t_done")
        y_ready = sem("y_ready")
        y_done = sem("y_done")
        stats1_done = sem("stats1_done")
        var1_done = sem("var1_done")
        rstd1_done = sem("rstd1_done")
        xn_done = sem("xn_done")
        stats2_done = sem("stats2_done")
        var2_done = sem("var2_done")
        rstd2_done = sem("rstd2_done")
        xn2_done = sem("xn2_done")
        route_done = sem("route_done")
        exp_logit_done = sem("exp_logit_done")

        x_view = x.rearrange("b (c p) t -> b p c t", p=P)
        ctx_view = ctx_in.rearrange("b (c p) t -> b p c t", p=P)
        out_view = out.rearrange("b (c p) t -> b p c t", p=P)

        loads = [(wq_sb, wq_t), (bq_sb, bq), (wk_sb, wk_t), (bk_sb, bk), (wv_sb, wv_t), (wo_sb, wo_t),
                 (bo_sb, bo), (a_sb, a_t), (b_sb, b_t), (wr_sb, wr_t), (br_sb, br), (bv_sb, bv.partition_broadcast(P))]
        all_weights = 16 * len(loads)

        block = stack.enter_context(nc.Block())

        @block.sync
        def _(sp):
            def load_x(b):
                sp.dma_start(x_raw[:, :, :], x_view[b, :, :, :]).then_inc(x_in, 16)

            def load_ctx(b):
                sp.dma_start(ctx_sb[:, :, :], ctx_view[b, :, :, :]).then_inc(ctx_in_sem, 16)

            def stack_quad(b, q):
                c = q // 2
                sp.wait_ge(qk_lo_done, b * 4 + (2 * c + 2))
                stand_alone(sp, passed)
                if counts(b * UNITS + (16 * q + 16 - UNITS)):
                    sp.wait_ge(s2_ready, b * UNITS + (16 * q + 16 - UNITS))
                rows = slice(64 * (q % 2), 64 * (q % 2) + 64)
                heads = slice(4 * q, 4 * q + 4)
                for to, parts in ((q_stack, (q_hi, q_hi, q_lo)), (k_stack, (k_hi, k_lo, k_hi))):
                    for n, part in enumerate(parts):
                        sp.dma_start(to[16 * n:16 * n + 16, heads, :].bitcast(F32),
                                     part[rows, c, :].bitcast(F32)).then_inc(stack_in[q], 16)

            def stack_max(b, q):
                sp.wait_ge(max_lo_done, b * 4 + (q + 1))
                for n in range(2):
                    row = SPLIT_ROWS + n
                    sp.dma_start(q_stack[row:row + 1, 4 * q:4 * q + 4, :].bitcast(F32),
                                 max_rows[:, n, :].bitcast(F32)).then_inc(max_rows_in[q], 16)

            def store(b, t):
                sp.wait_ge(y_done, b * 2 + (t + 1))
                stand_alone(sp, passed)
                sp.dma_start(out_view[b, :, t, :], y_out[:, t, :]).then_inc(out_stored[t], 16)

            load_x(0)
            load_ctx(0)
            for to, src in loads:
                sp.dma_start(to[(slice(None),) * len(to.shape)], src).then_inc(weights_in, 16)
            sp.wait_ge(pad_set, 2)
            sp.wait_ge(ones_set, 1)

            def iteration(it):
                b = it.b
                if it.live(0):
                    stack_quad(b, 1)
                if it.live(-1):
                    stack_max(b - 1, 3)
                if it.live(0):
                    stack_quad(b, 2)
                if it.live(2):
                    sp.wait_ge(xn_done, b * 2 + 4)
                    stand_alone(sp, passed)
                    load_x(b + 2)
                if it.live(0):
                    stack_max(b, 0)
                    stack_quad(b, 3)
                if it.live(-2):
                    store(b - 2, 0)
                if it.live(0):
                    stack_max(b, 1)
                if it.live(-2):
                    store(b - 2, 1)
                if it.live(1):
                    stack_quad(b + 1, 0)
                if it.live(0):
                    if counts(b * 2):
                        sp.wait_ge(x2_done, b * 2)
                    stand_alone(sp, passed)
                    sp.dma_start(x_again[:, :, :], x_view[b, :, :, :]).then_inc(x_again_in, 16)
                    stack_max(b, 2)
                if it.live(2):
                    sp.wait_ge(v_ready, b * 2 + 4)
                    stand_alone(sp, passed)
                    load_ctx(b + 2)

            run_iterations(sp, iteration)
            for t in range(CH):
                sp.wait_ge(out_stored[t], 16 * BATCHES)

        @block.gpsimd
        def _(pool):
            nc.gpsimd.memset(ident[:, :], 0.0).then_inc(ident_set, 1)
            nc.gpsimd.memset(v_ones[:, :, :, :, :], 0.0).then_inc(ident_set, 1)
            for e in range(E):
                last = nc.gpsimd.memset(rank[:, :, e:e + 1], float(E - e))
            last.then_inc(ident_set, 1)
            nc.gpsimd.memset(minus_half[:, :], -0.5).then_inc(ident_set, 1)
            pool.wait_ge(ident_set, 4)
            nc.gpsimd.affine_select(out=ident[:, :], in_=ident[:, :], compare_op=ALU.not_equal, fill=1.0, base=0,
                                    pattern=[[-1, P]], channel_multiplier=1).then_inc(ident_set, 1)
            for q in range(QUADS):
                last = nc.gpsimd.memset(v_ones[:, q, :, :, 16:17], 1.0)
            last.then_inc(ident_set, 1)
            pool.wait_ge(ident_set, 6)
            nc.gpsimd.memset(k_stack[SPLIT_ROWS:FULL_ROWS, :, :].bitcast(F32), 1.0).then_inc(ones_set, 1)
            pool.wait_ge(ones_set, 1)

            def copy_v(b, q):
                pool.wait_ge(v_plain_done, b * 2 + 2)
                if counts(b * STEPS + (4 * q + 4 - STEPS)):
                    pool.wait_ge(pv_done, b * STEPS + (4 * q + 4 - STEPS))
                stand_alone(pool, passed)
                nc.gpsimd.tensor_copy(
                    v_ones[:, q, :, :, 0:KC],
                    v_plain[:, :, 64 * q:64 * q + 64].rearrange("p s (i k) -> p s i k", k=KC),
                ).then_inc(v_ones_done, 1)

            def root(b, stats, mean_var, var_eps, rstd, stats_sem, need, var_sem, var_count, rstd_sem):
                pool.wait_ge(stats_sem, need)
                stand_alone(pool, passed)
                nc.gpsimd.tensor_scalar(var_eps, mean_var, EPS, None, ALU.add).then_inc(var_sem, 1)
                pool.wait_ge(var_sem, var_count)
                nc.gpsimd.tensor_tensor(rstd, var_eps, minus_half[:, 0:rstd.shape[1]],
                                        ALU.pow).then_inc(rstd_sem, 1)

            def iteration(it):
                b = it.b
                if it.live(0):
                    copy_v(b, 0)
                    copy_v(b, 1)
                if it.live(1):
                    root(b + 1, stats1, mean_var1[:, :, 1], var_eps1[:, :], rstd1[:, :], stats1_done,
                         b * 4 + 8, var1_done, b + 2, rstd1_done)
                if it.live(0):
                    copy_v(b, 2)
                    copy_v(b, 3)
                if it.live(-1):
                    for c in range(CH):
                        root(b - 1, stats2, mean_var2[:, c:c + 1, 1], var_eps2[:, c:c + 1], rstd2[:, c:c + 1],
                             stats2_done, b * 4 + (2 * c - 2), var2_done, b * 2 + (c - 1), rstd2_done)

            run_iterations(pool, iteration)

        @block.scalar
        def _(act):
            def exps(batch, step, i):
                act.wait_ge(s2_ready, batch * UNITS + (4 * step + i + 1))
                if i == 0:
                    if counts(batch * STEPS + (step - 1)):
                        act.wait_ge(pv_done, batch * STEPS + (step - 1))
                nc.scalar.activation(probs[:, step % 2, i, :], s2_bank[i % 2][:, :], ACT.Exp,
                                     scale=SCALE).then_inc(exp_done, 1)

            def high_part(batch, name, hi, bias, chunk, n):
                act.wait_ge(qk_ready, batch * 4 + (n + 1))
                for q in (2 * chunk, 2 * chunk + 1):
                    if counts(batch * 96):
                        act.wait_ge(stack_in[q], batch * 96)
                nc.scalar.activation(hi[:, chunk, :], bank_of[name][:, :], ACT.Identity,
                                     bias=bias[:, chunk:chunk + 1]).then_inc(qk_hi_done, 1)

            def max_high(batch, q):
                act.wait_ge(max_turned, batch * 4 + (q + 1))
                if q:
                    act.wait_ge(max_rows_in[q - 1], batch * 32 + 32)
                else:
                    if counts(batch * 32):
                        act.wait_ge(max_rows_in[QUADS - 1], batch * 32)
                nc.scalar.copy(max_rows[:, 0, :], bank_of[f"max{q}"][0:4, :]).then_inc(max_hi_done, 1)

            def x_turn(batch, t):
                act.wait_ge(x_turned, batch * 2 + (t + 1))
                if counts(batch * 2):
                    act.wait_ge(hidden_ready, batch * 2)
                nc.scalar.copy(xn2_t[:, t, :, :].rearrange("p d r -> p (d r)"),
                               bank_of[f"x_turn{t}"][:, :]).then_inc(xn2_t_done, 1)

            def hidden_turn(batch, t):
                act.wait_ge(hidden_turned, batch * 2 + (t + 1))
                if counts(batch * 2):
                    act.wait_ge(y_ready, batch * 2)
                nc.scalar.copy(hidden_t[:, t, :, :].rearrange("p d r -> p (d r)"),
                               bank_of[f"hidden_turn{t}"][:, :]).then_inc(hidden_t_done, 1)

            def logits_out(batch):
                act.wait_ge(logits_ready, batch + 1)
                if counts(batch):
                    act.wait_ge(logit_turned, batch)
                nc.scalar.activation(logits_t[:, :], bank_of["logits"][0:E, 0:CH * P], ACT.Identity,
                                     bias=br_sb[:, 0:1]).then_inc(logits_t_done, 1)

            def logit_exp(batch):
                act.wait_ge(route_done, batch * ROUTE + 3)
                nc.scalar.activation(exp_logit[:, :, :], below_top[:, :, :], ACT.Exp).then_inc(exp_logit_done, 1)

            def iteration(it):
                b = it.b
                for s in range(STEPS):
                    for i in range(5):
                        if (s, i) == (0, 0) and it.live(-2):
                            logits_out(b - 2)
                        if (s, i) == (1, 1) and it.live(-2):
                            logit_exp(b - 2)
                        if (s, i) == (1, 3) and it.live(-1):
                            max_high(b - 1, 3)
                        if (s, i) == (3, 4) and it.live(-2):
                            hidden_turn(b - 2, 0)
                        if (s, i) == (4, 3) and it.live(1):
                            high_part(b + 1, "q0", q_hi, bq_sb, 0, 0)
                        if s in (5, 9, 13) and i == 2 and it.live(0):
                            max_high(b, (s - 5) // 4)
                        if (s, i) == (5, 4) and it.live(1):
                            high_part(b + 1, "k0", k_hi, bk_sb, 0, 1)
                        if (s, i) == (6, 2) and it.live(-2):
                            hidden_turn(b - 2, 1)
                        if (s, i) == (12, 4) and it.live(1):
                            high_part(b + 1, "q1", q_hi, bq_sb, 1, 2)
                        if (s, i) == (13, 4) and it.live(1):
                            high_part(b + 1, "k1", k_hi, bk_sb, 1, 3)
                        if (s, i) == (14, 4) and it.live(-1):
                            x_turn(b - 1, 0)
                        if (s, i) == (15, 2) and it.live(-1):
                            x_turn(b - 1, 1)
                        if i < 4 and s < LAG and it.live(-1):
                            exps(b - 1, s + LAG, i)
                        if i < 4 and s >= LAG and it.live(0):
                            exps(b, s - LAG, i)

            act.wait_ge(weights_in, all_weights)
            run_iterations(act, iteration)

        @block.vector
        def _(dve):
            nc.vector.memset(q_stack[0:SPLIT_ROWS, :, :].bitcast(F32), 0.0).then_inc(pad_set, 1)
            nc.vector.memset(k_stack[0:SPLIT_ROWS, :, :].bitcast(F32), 0.0).then_inc(pad_set, 1)

            def row_max(batch, q, piece, i):
                dve.wait_ge(s1_ready, batch * UNITS + (16 * q + 4 * piece + i + 1))
                nc.vector.tensor_reduce(neg_max[:, q, piece, i:i + 1], s1_bank[i % 2][:, :], X_AXIS, ALU.max,
                                        negate=True).then_inc(max_done, 1)

            def max_low(batch, q):
                dve.wait_ge(max_hi_done, batch * 4 + (q + 1))
                nc.vector.tensor_tensor(max_rows[:, 1, :], bank_of[f"max{q}"][0:4, :], max_rows[:, 0, :],
                                        ALU.subtract).then_inc(max_lo_done, 1)

            def low_part(batch, name, hi, lo, bias, chunk, n):
                dve.wait_ge(qk_hi_done, batch * 4 + (n + 1))
                nc.vector.scalar_tensor_tensor(
                    out=lo[:, chunk, :], in0=bank_of[name][:, :], scalar=bias[:, chunk:chunk + 1],
                    in1=hi[:, chunk, :], op0=ALU.add, op1=ALU.subtract).then_inc(qk_lo_done, 1)

            def normalise(batch, q):
                first = batch * NORM + QUAD_NORM[q]
                if counts(first):
                    dve.wait_ge(norm_done, first)
                dve.wait_ge(pv_done, batch * STEPS + (4 * q + 4))
                nc.vector.transpose(turned[:, :, :].rearrange("p n k -> p (n k)"),
                                    pv_bank[q % 2][:, :]).then_inc(norm_done, 1)
                dve.wait_ge(norm_done, first + 1)
                nc.vector.reciprocal(inv_sum[:, :, :], turned[:, :, KC:KC + 1]).then_inc(norm_done, 1)
                dve.wait_ge(norm_done, first + 2)
                half = slice(KC * (q % 2), KC * (q % 2) + KC)
                nc.vector.tensor_tensor(normed[:, :, half], turned[:, :, 0:KC],
                                        inv_sum[:, :, :].to_broadcast([P, BLOCKS, KC]),
                                        ALU.mult).then_inc(norm_done, 1)
                if q % 2:
                    dve.wait_ge(norm_done, first + 3)
                    if counts(batch * 2):
                        dve.wait_ge(out_ready, batch * 2)
                    nc.vector.transpose(heads_out[:, q // 2, :],
                                        normed[:, :, :].rearrange("p n k -> p (n k)")).then_inc(norm_done, 1)

            def statistics(batch, c, source, stats, mean_var, done):
                nc.vector.bn_stats(stats[:, c, :], source[:, c, :]).then_inc(done, 1)
                dve.wait_ge(done, batch * 4 + (2 * c + 1))
                stand_alone(dve, passed)
                nc.vector.bn_aggr(mean_var[:, c, :], stats[:, c, :]).then_inc(done, 1)

            def scale_rows(c, to, source, mean_var, rstd, done):
                nc.vector.tensor_scalar(to[:, c, :], source[:, c, :], mean_var[:, c, 0:1], rstd[:, c:c + 1],
                                        ALU.subtract, ALU.mult).then_inc(done, 1)

            def statistics1(batch):
                dve.wait_ge(x_in, batch * 16 + 16)
                for c in range(CH):
                    statistics(batch, c, x_raw, stats1, mean_var1, stats1_done)

            def layernorm1(batch):
                dve.wait_ge(rstd1_done, batch + 1)
                if counts(batch * 4 - 1):
                    dve.wait_ge(qk_ready, batch * 4 - 1)
                for c in range(CH):
                    scale_rows(c, xn, x_raw, mean_var1, rstd1, xn_done)

            def v_add(batch, half):
                dve.wait_ge(v_ready, batch * 2 + (half + 1))
                if counts(batch * 4):
                    dve.wait_ge(v_ones_done, batch * 4)
                nc.vector.tensor_tensor(
                    v_plain[:, 2 * half:2 * half + 2, :],
                    bank_of[f"v{half}"][:, :].rearrange("p (s c) -> p s c", s=2),
                    bv_sb[:, :].unsqueeze(1).to_broadcast([P, 2, C]), ALU.add).then_inc(v_plain_done, 1)

            def residual(batch, c):
                dve.wait_ge(out_ready, batch * 2 + (c + 1))
                dve.wait_ge(x_again_in, batch * 16 + 16)
                nc.vector.scalar_tensor_tensor(
                    out=x2[:, c, :], in0=bank_of[f"out{c}"][:, :], scalar=bo_sb[:, c:c + 1],
                    in1=x_again[:, c, :], op0=ALU.add, op1=ALU.add).then_inc(x2_done, 1)
                dve.wait_ge(x2_done, batch * 2 + (c + 1))
                statistics(batch, c, x2, stats2, mean_var2, stats2_done)

            def layernorm2(batch, c):
                dve.wait_ge(rstd2_done, batch * 2 + (c + 1))
                if counts(batch * 2):
                    dve.wait_ge(x_turned, batch * 2)
                scale_rows(c, xn2, x2, mean_var2, rstd2, xn2_done)

            def route_start(batch):
                n = batch * ROUTE
                wide = [P, CH, E]
                dve.wait_ge(logit_turned, batch + 1)
                nc.vector.tensor_copy(logit[:, :, :],
                                      bank_of["logit_turn"][:, 0:CH * E].rearrange("p (t e) -> p t e", t=CH)
                                      ).then_inc(route_done, 1)
                dve.wait_ge(route_done, n + 1)
                nc.vector.tensor_reduce(top[:, :, :], logit[:, :, :], X_AXIS, ALU.max).then_inc(route_done, 1)
                dve.wait_ge(route_done, n + 2)
                nc.vector.tensor_tensor(below_top[:, :, :], logit[:, :, :], top[:, :, :].to_broadcast(wide),
                                        ALU.subtract).then_inc(route_done, 1)
                nc.vector.tensor_tensor(is_top[:, :, :], logit[:, :, :], top[:, :, :].to_broadcast(wide),
                                        ALU.is_equal).then_inc(route_done, 1)

            def route_end(batch):
                n = batch * ROUTE
                wide = [P, CH, E]
                dve.wait_ge(route_done, n + 4)
                nc.vector.tensor_tensor(top_rank[:, :, :], is_top[:, :, :], rank[:, :, :],
                                        ALU.mult).then_inc(route_done, 1)
                dve.wait_ge(route_done, n + 5)
                nc.vector.tensor_reduce(best_rank[:, :, :], top_rank[:, :, :], X_AXIS,
                                        ALU.max).then_inc(route_done, 1)
                dve.wait_ge(route_done, n + 6)
                nc.vector.tensor_tensor(chosen[:, :, :], top_rank[:, :, :], best_rank[:, :, :].to_broadcast(wide),
                                        ALU.is_equal).then_inc(route_done, 1)
                dve.wait_ge(exp_logit_done, batch + 1)
                nc.vector.tensor_reduce(exp_sum[:, :, :], exp_logit[:, :, :], X_AXIS,
                                        ALU.add).then_inc(route_done, 1)
                dve.wait_ge(route_done, n + 8)
                nc.vector.reciprocal(weight[:, :, :], exp_sum[:, :, :]).then_inc(route_done, 1)
                dve.wait_ge(route_done, n + 9)
                nc.vector.scalar_tensor_tensor(
                    out=gate[:, :, :], in0=chosen[:, :, :], scalar=1.0 / R, in1=weight[:, :, :].to_broadcast(wide),
                    op0=ALU.mult, op1=ALU.mult).then_inc(route_done, 1)

            def gate_hidden(batch, t):
                dve.wait_ge(route_done, batch * ROUTE + ROUTE)
                dve.wait_ge(hidden_ready, batch * 2 + (t + 1))
                if counts(batch * 2):
                    dve.wait_ge(hidden_turned, batch * 2)
                nc.vector.tensor_tensor(
                    hidden[:, t, :].rearrange("p (e r) -> p e r", e=E),
                    bank_of[f"hidden{t}"][:, :].rearrange("p (e r) -> p e r", e=E),
                    gate[:, t, :].unsqueeze(2).to_broadcast([P, E, R]), ALU.mult).then_inc(hidden_done, 1)

            def result(batch, t):
                dve.wait_ge(y_ready, batch * 2 + (t + 1))
                if counts(batch * 16):
                    dve.wait_ge(out_stored[t], batch * 16)
                nc.vector.tensor_tensor(y_out[:, t, :], bank_of[f"y{t}"][:, :], x2[:, t, :],
                                        ALU.add).then_inc(y_done, 1)

            def iteration(it):
                b = it.b
                for s in range(STEPS):
                    for i in range(4):
                        if it.live(0):
                            row_max(b, s // PIECES, s % PIECES, i)
                        if (s, i) == (0, 3) and it.live(-2):
                            route_start(b - 2)
                        if (s, i) == (1, 1) and it.live(-1):
                            normalise(b - 1, 1)
                        if (s, i) == (1, 3) and it.live(-2):
                            route_end(b - 2)
                        if (s, i) == (2, 0) and it.live(-2):
                            gate_hidden(b - 2, 0)
                        if (s, i) == (2, 1) and it.live(-1):
                            max_low(b - 1, 3)
                        if (s, i) == (2, 3) and it.live(1):
                            statistics1(b + 1)
                        if (s, i) == (3, 3) and it.live(-2):
                            gate_hidden(b - 2, 1)
                        if (s, i) == (3, 3) and it.live(1):
                            layernorm1(b + 1)
                        if (s, i) == (5, 0) and it.live(1):
                            low_part(b + 1, "q0", q_hi, q_lo, bq_sb, 0, 0)
                        if (s, i) == (5, 2) and it.live(-1):
                            normalise(b - 1, 2)
                        if (s, i) == (6, 0) and it.live(1):
                            low_part(b + 1, "k0", k_hi, k_lo, bk_sb, 0, 1)
                        if s in (5, 9, 13) and i == 3 and it.live(0):
                            max_low(b, (s - 5) // 4)
                        if (s, i) == (8, 0) and it.live(-2):
                            result(b - 2, 0)
                        if (s, i) == (9, 0) and it.live(-1):
                            normalise(b - 1, 3)
                        if (s, i) == (10, 0) and it.live(-2):
                            result(b - 2, 1)
                        if (s, i) == (11, 0) and it.live(1):
                            v_add(b + 1, 0)
                        if (s, i) == (12, 0) and it.live(-1):
                            residual(b - 1, 0)
                        if (s, i) == (12, 2) and it.live(-1):
                            residual(b - 1, 1)
                        if (s, i) == (13, 0) and it.live(1):
                            low_part(b + 1, "q1", q_hi, q_lo, bq_sb, 1, 2)
                        if (s, i) == (13, 1) and it.live(-1):
                            layernorm2(b - 1, 0)
                        if (s, i) == (13, 2) and it.live(0):
                            normalise(b, 0)
                        if (s, i) == (13, 3) and it.live(-1):
                            layernorm2(b - 1, 1)
                        if (s, i) == (14, 0) and it.live(1):
                            low_part(b + 1, "k1", k_hi, k_lo, bk_sb, 1, 3)
                        if (s, i) == (15, 0) and it.live(1):
                            v_add(b + 1, 1)

            dve.wait_ge(weights_in, all_weights)
            dve.wait_ge(ident_set, 6)
            run_iterations(dve, iteration)

        @block.tensor
        def _(pe):
            def scores_for_max(batch, s, i):
                q, head, rows = s // PIECES, 4 * (s // PIECES) + i, slice(P * (s % PIECES), P * (s % PIECES) + P)
                if s % PIECES == 0 and i == 0:
                    pe.wait_ge(stack_in[q], batch * 96 + 96)
                if counts(batch * UNITS + (4 * s + i - 1)):
                    pe.wait_ge(max_done, batch * UNITS + (4 * s + i - 1))
                nc.tensor.matmul(s1_bank[i % 2][:, :], q_stack[0:SPLIT_ROWS, head, rows],
                                 k_stack[0:SPLIT_ROWS, head, :], start=True, stop=True).then_inc(s1_ready, 1)

            def scores_less_max(batch, s, i):
                q, head, rows = s // PIECES, 4 * (s // PIECES) + i, slice(P * (s % PIECES), P * (s % PIECES) + P)
                if s % PIECES == 0 and i == 0:
                    pe.wait_ge(max_rows_in[q], batch * 32 + 32)
                if counts(batch * UNITS + (4 * s + i - 1)):
                    pe.wait_ge(exp_done, batch * UNITS + (4 * s + i - 1))
                nc.tensor.matmul(s2_bank[i % 2][:, :], k_stack[0:FULL_ROWS, head, rows],
                                 q_stack[0:FULL_ROWS, head, :], start=True, stop=True).then_inc(s2_ready, 1)

            def probs_times_v(batch, s):
                q, piece = s // PIECES, s % PIECES
                if piece == 0:
                    pe.wait_ge(v_ones_done, batch * 4 + (q + 1))
                    last = QUAD_NORM[q - 2] if q >= 2 else QUAD_NORM[q + 2] - NORM
                    if counts(batch * NORM + (last + 1)):
                        pe.wait_ge(norm_done, batch * NORM + (last + 1))
                pe.wait_ge(exp_done, batch * UNITS + (4 * s + 4))
                for i in range(4):
                    last = nc.tensor.matmul(pv_bank[q % 2][32 * i:32 * i + 32, :], v_ones[:, q, piece, i, :],
                                            probs[:, s % 2, i, :], start=piece == 0, stop=piece == PIECES - 1)
                last.then_inc(pv_done, 1)

            def project(it, name, weights, source, c, kc):
                return nc.tensor.matmul(bank_of[name][:, :], weights[:, kc, P * c:P * c + P], source[:, kc, :],
                                        start=kc == 0, stop=kc == CH - 1)

            def query(it, c, kc):
                b = it.b
                if kc == 0:
                    if c == 0 and it.live(-2):
                        pe.wait_ge(hidden_done, b * 2 - 2)
                    elif c == 0 and it.live(0):
                        pe.wait_ge(qk_lo_done, b * 4 + 4)
                    elif c == 1 and it.live(-1):
                        pe.wait_ge(x2_done, b * 2 - 1)
                    elif c == 1 and it.live(0):
                        pe.wait_ge(max_lo_done, b * 4 + 2)
                    elif c == 1:
                        pe.wait_ge(qk_lo_done, b * 4 + 6)
                    pe.wait_ge(xn_done, b * 2 + 4)
                last = project(it, f"q{c}", wq_sb, xn, c, kc)
                if kc == CH - 1:
                    last.then_inc(qk_ready, 1)

            def key(it, c, kc):
                b = it.b
                if kc == 0:
                    pe.wait_ge(qk_lo_done, b * 4 + (5 + 2 * c))
                    pe.wait_ge(ctx_in_sem, b * 16 + 32)
                last = project(it, f"k{c}", wk_sb, ctx_sb, c, kc)
                if kc == CH - 1:
                    last.then_inc(qk_ready, 1)

            def value(it, half, n):
                b = it.b
                if n == 0:
                    if half == 0 and it.live(-2):
                        pe.wait_ge(y_done, b * 2 - 2)
                    elif half == 0 and it.live(0):
                        pe.wait_ge(max_lo_done, b * 4 + 1)
                    elif half == 1 and it.live(0):
                        pe.wait_ge(max_lo_done, b * 4 + 3)
                    elif half == 1:
                        pe.wait_ge(v_plain_done, b * 2 + 3)
                rows = slice(P * (2 * half + n), P * (2 * half + n) + P)
                for kc in range(CH):
                    last = nc.tensor.matmul(bank_of[f"v{half}"][:, C * n:C * n + C], ctx_sb[:, kc, rows],
                                            wv_sb[:, kc, :], start=kc == 0, stop=kc == CH - 1)
                if n == 1:
                    last.then_inc(v_ready, 1)

            def output(it, c, kc):
                b = it.b
                if kc == 0:
                    if c == 0 and it.live(0):
                        pe.wait_ge(max_lo_done, b * 4 + 2)
                    elif c == 0:
                        pe.wait_ge(y_done, b * 2 - 3)
                    elif it.live(1):
                        pe.wait_ge(v_plain_done, b * 2 + 3)
                    else:
                        pe.wait_ge(y_done, b * 2 - 2)
                    pe.wait_ge(norm_done, b * NORM)
                last = project(it, f"out{c}", wo_sb, heads_out, c, kc)
                if kc == CH - 1:
                    last.then_inc(out_ready, 1)

            def turn_max(it, off, q):
                b = it.b
                if q == 3 and it.live(-2):
                    pe.wait_ge(route_done, b * ROUTE + (1 - 2 * ROUTE))
                elif q == 3:
                    pe.wait_ge(v_plain_done, b * 2 + 2)
                elif q == 0 and it.live(-2):
                    pe.wait_ge(hidden_t_done, b * 2 - 3)
                elif q == 0 and it.live(-1):
                    pe.wait_ge(max_lo_done, b * 4)
                elif q == 0:
                    pe.wait_ge(v_plain_done, b * 2 + 2)
                elif q == 1 and it.live(-2):
                    pe.wait_ge(y_done, b * 2 - 3)
                elif q == 1:
                    pe.wait_ge(qk_lo_done, b * 4 + 6)
                elif it.live(-1):
                    pe.wait_ge(x2_done, b * 2)
                else:
                    pe.wait_ge(v_plain_done, b * 2 + 3)
                pe.wait_ge(max_done, (b + off) * UNITS + (16 * q + 16))
                for piece in range(PIECES):
                    last = nc.tensor.matmul(bank_of[f"max{q}"][0:4, P * piece:P * piece + P],
                                            neg_max[:, q, piece, :], ident[:, :], start=True, stop=True)
                last.then_inc(max_turned, 1)

            def turn_x(it, t):
                b = it.b
                if t == 0 and it.live(1):
                    pe.wait_ge(qk_lo_done, b * 4 + 8)
                elif t == 1 and it.live(1):
                    pe.wait_ge(v_plain_done, b * 2 + 4)
                elif t == 1 and it.live(0):
                    pe.wait_ge(max_lo_done, b * 4 + 3)
                pe.wait_ge(xn2_done, b * 2 + (t - 1))
                for d in range(DCH):
                    last = nc.tensor.transpose(bank_of[f"x_turn{t}"][:, P * d:P * d + P],
                                               xn2[:, t, P * d:P * d + P], ident[:, :])
                last.then_inc(x_turned, 1)

            def router(it, half):
                b = it.b
                if half == 0:
                    pe.wait_ge(xn2_t_done, b * 2)
                for d in (2 * half, 2 * half + 1):
                    last = nc.tensor.matmul(bank_of["logits"][0:E, 0:CH * P], wr_sb[:, d, :], xn2_t[:, :, d, :],
                                            start=d == 0, stop=d == DCH - 1)
                if half == 1:
                    last.then_inc(logits_ready, 1)

            def turn_logits(it):
                b = it.b
                pe.wait_ge(logits_t_done, b - 1)
                stand_alone(pe, passed)
                for t in range(CH):
                    last = nc.tensor.transpose(bank_of["logit_turn"][:, E * t:E * t + E],
                                               logits_t[:, P * t:P * t + P], ident[0:E, 0:E])
                last.then_inc(logit_turned, 1)

            def expert_in(it, t, d):
                b = it.b
                if d == 0:
                    if t == 1:
                        pe.wait_ge(hidden_done, b * 2 - 3)
                last = nc.tensor.matmul(bank_of[f"hidden{t}"][:, :], xn2_t[:, t, d, :], a_sb[:, d, :],
                                        start=d == 0, stop=d == DCH - 1)
                if d == DCH - 1:
                    last.then_inc(hidden_ready, 1)

            def turn_hidden(it, t):
                b = it.b
                if t == 0 and it.live(-1):
                    pe.wait_ge(max_lo_done, b * 4)
                elif t == 1 and it.live(0):
                    pe.wait_ge(max_lo_done, b * 4 + 1)
                elif t == 1:
                    pe.wait_ge(hidden_t_done, b * 2 - 3)
                pe.wait_ge(hidden_done, b * 2 + (t - 3))
                for d in range(DCH):
                    last = nc.tensor.transpose(bank_of[f"hidden_turn{t}"][:, P * d:P * d + P],
                                               hidden[:, t, P * d:P * d + P], ident[:, :])
                last.then_inc(hidden_turned, 1)

            def expert_out(it, t, d):
                b = it.b
                if d == 0:
                    if t == 0 and it.live(1):
                        pe.wait_ge(qk_lo_done, b * 4 + 6)
                    pe.wait_ge(hidden_t_done, b * 2 + (t - 3))
                last = nc.tensor.matmul(bank_of[f"y{t}"][:, :], hidden_t[:, t, d, :], b_sb[:, d, :],
                                        start=d == 0, stop=d == DCH - 1)
                if d == DCH - 1:
                    last.then_inc(y_ready, 1)

            def beside(it, s, i):
                if it.live(-2):
                    if (s, i) == (0, 1):
                        turn_logits(it)
                    if s == 0 and i >= 2:
                        expert_in(it, 0, i - 2)
                if it.live(-1) and (s, i) == (1, 0):
                    turn_max(it, -1, 3)
                if it.live(-2):
                    if s == 1 and i in (1, 2):
                        expert_in(it, 0, i + 1)
                    if s in (2, 3) and i < 2:
                        expert_in(it, 1, 2 * (s - 2) + i)
                    if (s, i) == (3, 2):
                        turn_hidden(it, 0)
                if it.live(1) and s == 4 and i < 2:
                    query(it, 0, i)
                if it.live(0) and s in (5, 9, 13) and i == 0:
                    turn_max(it, 0, (s - 5) // 4)
                if it.live(1) and s == 5 and i in (1, 2):
                    key(it, 0, i - 1)
                if it.live(-2):
                    if (s, i) == (6, 0):
                        turn_hidden(it, 1)
                    if s == 6 and i in (1, 2):
                        expert_out(it, 0, i - 1)
                    if s == 7 and i < 2:
                        expert_out(it, 0, i + 2)
                    if s == 8 and i < 2:
                        expert_out(it, 1, i)
                    if s == 9 and i in (1, 2):
                        expert_out(it, 1, i + 1)
                if it.live(1) and s == 10 and i < 2:
                    value(it, 0, i)
                if it.live(-1):
                    if s == 11 and i < 3:
                        output(it, i // 2, i % 2)
                    if (s, i) == (12, 0):
                        output(it, 1, 1)
                if it.live(1):
                    if s == 12 and i in (1, 2):
                        query(it, 1, i - 1)
                    if s == 13 and i in (1, 2):
                        key(it, 1, i - 1)
                    if s == 14 and i < 2:
                        value(it, 1, i)
                if it.live(-1):
                    if (s, i) == (14, 2):
                        turn_x(it, 0)
                    if (s, i) == (15, 0):
                        turn_x(it, 1)
                    if s == 15 and i in (1, 2):
                        router(it, i - 1)

            def iteration(it):
                b = it.b
                for s in range(STEPS):
                    for i in range(4):
                        if it.live(0):
                            scores_for_max(b, s, i)
                        if s < LAG and it.live(-1):
                            scores_less_max(b - 1, s + LAG, i)
                        if s >= LAG and it.live(0):
                            scores_less_max(b, s - LAG, i)
                        if i == 2:
                            if s <= LAG and it.live(-1):
                                probs_times_v(b - 1, s + LAG - 1)
                            if s > LAG and it.live(0):
                                probs_times_v(b, s - LAG - 1)
                        beside(it, s, i)

            pe.wait_ge(weights_in, all_weights)
            pe.wait_ge(ident_set, 6)
            run_iterations(pe, iteration)


def kernel(**inputs):
    import numpy as np
    import concourse.bacc as bacc
    from concourse.bass_utils import run_bass_kernel_spmd

    a = {name: np.asarray(value) for name, value in inputs.items()}
    x, ctx = a["x"], a["ctx_2048"]

    def columns(w):
        return w.reshape(w.shape[0], -1, P).transpose(2, 1, 0)

    def by_quad(w):
        return w.reshape(QUADS, 4, KC, -1).transpose(0, 2, 1, 3).reshape(HEADS * KC, -1)

    def chunks(v):
        return v.reshape(CH, P).transpose(1, 0)

    wo = a["L0_xattn_Wo"].reshape(C, CH, 2, 4, KC).transpose(3, 2, 4, 1, 0).reshape(P, CH, C)
    expert_b = a["L0_ffn_B"].transpose(0, 2, 1).reshape(DCH, P, D).transpose(1, 0, 2)
    arrays = {
        "x": x, "ctx_in": ctx,
        "wq_t": columns(by_quad(a["L0_xattn_Wq"])), "wk_t": columns(by_quad(a["L0_xattn_Wk"])),
        "wv_t": columns(a["L0_xattn_Wv"]), "wo_t": wo,
        "bq": chunks(by_quad(a["L0_xattn_bq"])), "bk": chunks(by_quad(a["L0_xattn_bk"])),
        "bv": a["L0_xattn_bv"], "bo": chunks(a["L0_xattn_bo"]),
        "a_t": columns(a["L0_ffn_A"].reshape(E * R, D)), "b_t": expert_b,
        "wr_t": columns(a["L0_ffn_Wr"]), "br": a["L0_ffn_br"].reshape(E, 1),
    }
    arrays = {f"{name}_dram": np.ascontiguousarray(value) for name, value in arrays.items()}
    nc = bacc.Bacc("TRN2", target_bir_lowering=False, num_devices=1)
    args = [nc.dram_tensor(name, v.shape, mybir.dt.from_np(v.dtype), kind="ExternalInput").ap()
            for name, v in arrays.items()]
    args.append(nc.dram_tensor("out_dram", (BATCHES, C, T), F32, kind="ExternalOutput").ap())
    xattn_experts(nc, *args)
    r = run_bass_kernel_spmd(nc, [arrays], core_ids=[0])
    return r.results[0]["out_dram"]
```

```python
from contextlib import ExitStack

import concourse.bass as bass
from concourse import mybir

F32 = mybir.dt.float32
F32R = mybir.dt.float32r
ALU = mybir.AluOpType
ACT = mybir.ActivationFunctionType
X_AXIS = mybir.AxisListType.X

P = 128
BATCHES, C, T = 16, 256, 512
HEADS, KC = 16, 16
SCALE = float(KC) ** -0.5
E, R, D = 8, 64, 512
EPS = 1e-5

CH = C // P
DCH = D // P
QUADS = HEADS // 4
PIECES = T // P
STEPS = QUADS * PIECES
LAG = STEPS // 2
UNITS = 4 * STEPS
SPLIT_ROWS = 96
FULL_ROWS = SPLIT_ROWS + 2
NORM = 14
QUAD_NORM = [0, 3, 7, 10]
ROUTE = 10
BLOCKS = T // 32

BANK_TURNS = [
    ("hidden1", "y0", "q0", "q1", "k1", "logits"),
    ("hidden_turn0", "hidden_turn1", "max0", "v0", "out0", "v1", "max2", "hidden0"),
    ("max3", "y1", "k0", "max1", "out1", "x_turn0", "x_turn1", "logit_turn"),
]
FIRST_TILE_OUT = [(1, 2), (2, 0), (2, 2), (3, 0)]
SECOND_TILE_OUT = [(3, 2), (4, 0), (4, 2), (5, 1)]
FIRST_FULL, LAST_FULL = 3, BATCHES - 3


class Iteration:

    def __init__(self, b, looped=False):
        self.b, self.looped = b, looped

    def live(self, offset):
        return self.looped or 0 <= self.b + offset < BATCHES


def counts(n):
    return not isinstance(n, int) or n > 0


def stand_alone(eng, sem):
    eng.sem_inc(sem, 1)


def run_iterations(eng, body):
    for b in range(-1, FIRST_FULL):
        body(Iteration(b))
    with eng.Fori(FIRST_FULL, LAST_FULL + 1) as b:
        body(Iteration(b, looped=True))
    for b in range(LAST_FULL + 1, BATCHES + 2):
        body(Iteration(b))


def xattn_experts(nc, x, ctx_in, wq_t, wk_t, wv_t, wo_t, bq, bk, bv, bo, a_t, b_t, wr_t, br, out):
    with ExitStack() as stack:
        def sb(name, shape, dt=F32):
            return stack.enter_context(nc.sbuf_tensor(name, shape, dt))

        def bank(name):
            return stack.enter_context(nc.psum_tensor(name, [P, 512], F32))

        def sem(name):
            return stack.enter_context(nc.semaphore(name))

        wq_sb = sb("wq_sb", [P, CH, C])
        wk_sb = sb("wk_sb", [P, CH, C])
        wv_sb = sb("wv_sb", [P, CH, C])
        wo_sb = sb("wo_sb", [P, CH, C])
        bq_sb = sb("bq_sb", [P, CH])
        bk_sb = sb("bk_sb", [P, CH])
        bv_sb = sb("bv_sb", [P, C])
        bo_sb = sb("bo_sb", [P, CH])
        a_sb = sb("a_sb", [P, DCH, E * R])
        b_sb = sb("b_sb", [P, DCH, D])
        wr_sb = sb("wr_sb", [P, DCH, E])
        br_sb = sb("br_sb", [E, 1])
        ident = sb("ident", [P, P])
        rank = sb("rank", [P, CH, E])
        minus_half = sb("minus_half", [P, CH])

        x_raw = sb("x_raw", [P, CH, T])
        ctx_sb = sb("ctx_sb", [P, CH, T])
        xn = sb("xn", [P, CH, T])
        q_hi = sb("q_hi", [P, CH, T], F32R)
        q_lo = sb("q_lo", [P, CH, T], F32R)
        k_hi = sb("k_hi", [P, CH, T], F32R)
        k_lo = sb("k_lo", [P, CH, T], F32R)
        q_stack = sb("q_stack", [P, HEADS, T], F32R)
        k_stack = sb("k_stack", [P, HEADS, T], F32R)
        neg_max = sb("neg_max", [P, QUADS, PIECES, 4])
        max_rows = sb("max_rows", [4, 2, T], F32R)
        probs = sb("probs", [P, 2, 4, T])
        v_plain = sb("v_plain", [P, PIECES, C])
        v_ones = sb("v_ones", [P, QUADS, PIECES, 4, 32])
        turned = sb("turned", [P, BLOCKS, 32])
        inv_sum = sb("inv_sum", [P, BLOCKS, 1])
        normed = sb("normed", [P, BLOCKS, 32])
        heads_out = sb("heads_out", [P, CH, T])

        x_again = sb("x_again", [P, CH, T])
        x2 = sb("x2", [P, CH, T])
        xn2 = sb("xn2", [P, CH, T])
        xn2_t = sb("xn2_t", [P, CH, DCH, P])
        stats1 = sb("stats1", [P, CH, 6])
        mean_var1 = sb("mean_var1", [P, CH, 2])
        var_eps1 = sb("var_eps1", [P, CH])
        rstd1 = sb("rstd1", [P, CH])
        stats2 = sb("stats2", [P, CH, 6])
        mean_var2 = sb("mean_var2", [P, CH, 2])
        var_eps2 = sb("var_eps2", [P, CH])
        rstd2 = sb("rstd2", [P, CH])
        logits_t = sb("logits_t", [E, CH * P])
        logit = sb("logit", [P, CH, E])
        top = sb("top", [P, CH, 1])
        below_top = sb("below_top", [P, CH, E])
        exp_logit = sb("exp_logit", [P, CH, E])
        exp_sum = sb("exp_sum", [P, CH, 1])
        weight = sb("weight", [P, CH, 1])
        is_top = sb("is_top", [P, CH, E])
        top_rank = sb("top_rank", [P, CH, E])
        best_rank = sb("best_rank", [P, CH, 1])
        chosen = sb("chosen", [P, CH, E])
        gate = sb("gate", [P, CH, E])
        hidden = sb("hidden", [P, CH, E * R])
        hidden_t = sb("hidden_t", [P, CH, DCH, P])
        y_out = sb("y_out", [P, CH, D])

        s1_bank = [bank(f"s1_bank{i}") for i in range(2)]
        s2_bank = [bank(f"s2_bank{i}") for i in range(2)]
        pv_bank = bank("pv_bank")
        bank_of = {}
        for k, turns in enumerate(BANK_TURNS):
            bank_of.update(dict.fromkeys(turns, bank(f"side_bank{k}")))

        weights_in = sem("weights_in")
        ones_set = sem("ones_set")
        pad_set = sem("pad_set")
        ident_set = sem("ident_set")
        passed = sem("passed")
        x_in = sem("x_in")
        ctx_in_sem = sem("ctx_in_sem")
        x_again_in = sem("x_again_in")
        stack_in = [sem(f"stack_in{q}") for q in range(QUADS)]
        max_rows_in = [sem(f"max_rows_in{q}") for q in range(QUADS)]
        out_stored = [sem(f"out_stored{t}") for t in range(CH)]
        s1_ready = sem("s1_ready")
        max_done = sem("max_done")
        s2_ready = sem("s2_ready")
        exp_done = sem("exp_done")
        pv_done = sem("pv_done")
        norm_done = sem("norm_done")
        qk_ready = sem("qk_ready")
        qk_hi_done = sem("qk_hi_done")
        qk_lo_done = sem("qk_lo_done")
        v_ready = sem("v_ready")
        v_plain_done = sem("v_plain_done")
        v_ones_done = sem("v_ones_done")
        max_turned = sem("max_turned")
        max_hi_done = sem("max_hi_done")
        max_lo_done = sem("max_lo_done")
        out_ready = sem("out_ready")
        x2_done = sem("x2_done")
        x_turned = sem("x_turned")
        xn2_t_done = sem("xn2_t_done")
        logits_ready = sem("logits_ready")
        logits_t_done = sem("logits_t_done")
        logit_turned = sem("logit_turned")
        hidden_ready = sem("hidden_ready")
        hidden_done = sem("hidden_done")
        hidden_turned = sem("hidden_turned")
        hidden_t_done = sem("hidden_t_done")
        y_ready = sem("y_ready")
        y_done = sem("y_done")
        stats1_done = sem("stats1_done")
        var1_done = sem("var1_done")
        rstd1_done = sem("rstd1_done")
        xn_done = sem("xn_done")
        stats2_done = sem("stats2_done")
        var2_done = sem("var2_done")
        rstd2_done = sem("rstd2_done")
        xn2_done = sem("xn2_done")
        route_done = sem("route_done")
        exp_logit_done = sem("exp_logit_done")

        x_view = x.rearrange("b (c p) t -> b p c t", p=P)
        ctx_view = ctx_in.rearrange("b (c p) t -> b p c t", p=P)
        out_view = out.rearrange("b (c p) t -> b p c t", p=P)

        loads = [(wq_sb, wq_t), (bq_sb, bq), (wk_sb, wk_t), (bk_sb, bk), (wv_sb, wv_t), (wo_sb, wo_t),
                 (bo_sb, bo), (a_sb, a_t), (b_sb, b_t), (wr_sb, wr_t), (br_sb, br), (bv_sb, bv.partition_broadcast(P))]
        all_weights = 16 * len(loads)

        block = stack.enter_context(nc.Block())

        @block.sync
        def _(sp):
            def load_x(b):
                sp.dma_start(x_raw[:, :, :], x_view[b, :, :, :]).then_inc(x_in, 16)

            def load_ctx(b):
                sp.dma_start(ctx_sb[:, :, :], ctx_view[b, :, :, :]).then_inc(ctx_in_sem, 16)

            def stack_quad(b, q):
                c = q // 2
                sp.wait_ge(qk_lo_done, b * 4 + (2 * c + 2))
                stand_alone(sp, passed)
                if counts(b * UNITS + (16 * q + 16 - UNITS)):
                    sp.wait_ge(s2_ready, b * UNITS + (16 * q + 16 - UNITS))
                rows = slice(64 * (q % 2), 64 * (q % 2) + 64)
                heads = slice(4 * q, 4 * q + 4)
                for to, parts in ((q_stack, (q_hi, q_hi, q_lo)), (k_stack, (k_hi, k_lo, k_hi))):
                    for n, part in enumerate(parts):
                        sp.dma_start(to[16 * n:16 * n + 16, heads, :].bitcast(F32),
                                     part[rows, c, :].bitcast(F32)).then_inc(stack_in[q], 16)

            def stack_max(b, q):
                sp.wait_ge(max_lo_done, b * 4 + (q + 1))
                for n in range(2):
                    row = SPLIT_ROWS + n
                    sp.dma_start(q_stack[row:row + 1, 4 * q:4 * q + 4, :].bitcast(F32),
                                 max_rows[:, n, :].bitcast(F32)).then_inc(max_rows_in[q], 16)

            def store(b, t):
                sp.wait_ge(y_done, b * 2 + (t + 1))
                stand_alone(sp, passed)
                sp.dma_start(out_view[b, :, t, :], y_out[:, t, :]).then_inc(out_stored[t], 16)

            load_x(0)
            load_ctx(0)
            for to, src in loads:
                sp.dma_start(to[(slice(None),) * len(to.shape)], src).then_inc(weights_in, 16)
            sp.wait_ge(pad_set, 2)
            sp.wait_ge(ones_set, 1)

            def iteration(it):
                b = it.b
                if it.live(0):
                    stack_quad(b, 1)
                if it.live(-1):
                    stack_max(b - 1, 3)
                if it.live(-2):
                    store(b - 2, 0)
                if it.live(0):
                    stack_quad(b, 2)
                if it.live(2):
                    sp.wait_ge(xn_done, b * 2 + 4)
                    stand_alone(sp, passed)
                    load_x(b + 2)
                if it.live(0):
                    stack_max(b, 0)
                if it.live(-2):
                    store(b - 2, 1)
                if it.live(0):
                    stack_quad(b, 3)
                    stack_max(b, 1)
                if it.live(1):
                    stack_quad(b + 1, 0)
                if it.live(0):
                    if counts(b * 2):
                        sp.wait_ge(x2_done, b * 2)
                    stand_alone(sp, passed)
                    sp.dma_start(x_again[:, :, :], x_view[b, :, :, :]).then_inc(x_again_in, 16)
                if it.live(2):
                    sp.wait_ge(v_ready, b * 2 + 4)
                    stand_alone(sp, passed)
                    load_ctx(b + 2)
                if it.live(0):
                    stack_max(b, 2)

            run_iterations(sp, iteration)
            for t in range(CH):
                sp.wait_ge(out_stored[t], 16 * BATCHES)

        @block.gpsimd
        def _(pool):
            nc.gpsimd.memset(ident[:, :], 0.0).then_inc(ident_set, 1)
            nc.gpsimd.memset(v_ones[:, :, :, :, :], 0.0).then_inc(ident_set, 1)
            for e in range(E):
                last = nc.gpsimd.memset(rank[:, :, e:e + 1], float(E - e))
            last.then_inc(ident_set, 1)
            nc.gpsimd.memset(minus_half[:, :], -0.5).then_inc(ident_set, 1)
            pool.wait_ge(ident_set, 4)
            nc.gpsimd.affine_select(out=ident[:, :], in_=ident[:, :], compare_op=ALU.not_equal, fill=1.0, base=0,
                                    pattern=[[-1, P]], channel_multiplier=1).then_inc(ident_set, 1)
            for q in range(QUADS):
                last = nc.gpsimd.memset(v_ones[:, q, :, :, 16:17], 1.0)
            last.then_inc(ident_set, 1)
            pool.wait_ge(ident_set, 6)
            nc.gpsimd.memset(k_stack[SPLIT_ROWS:FULL_ROWS, :, :].bitcast(F32), 1.0).then_inc(ones_set, 1)
            pool.wait_ge(ones_set, 1)

            def copy_v(b, q):
                pool.wait_ge(v_plain_done, b * 2 + 2)
                if counts(b * STEPS + (4 * q + 4 - STEPS)):
                    pool.wait_ge(pv_done, b * STEPS + (4 * q + 4 - STEPS))
                stand_alone(pool, passed)
                nc.gpsimd.tensor_copy(
                    v_ones[:, q, :, :, 0:KC],
                    v_plain[:, :, 64 * q:64 * q + 64].rearrange("p s (i k) -> p s i k", k=KC),
                ).then_inc(v_ones_done, 1)

            def root(b, stats, mean_var, var_eps, rstd, stats_sem, need, var_sem, var_count, rstd_sem):
                pool.wait_ge(stats_sem, need)
                stand_alone(pool, passed)
                nc.gpsimd.tensor_scalar(var_eps, mean_var, EPS, None, ALU.add).then_inc(var_sem, 1)
                pool.wait_ge(var_sem, var_count)
                nc.gpsimd.tensor_tensor(rstd, var_eps, minus_half[:, 0:rstd.shape[1]],
                                        ALU.pow).then_inc(rstd_sem, 1)

            def iteration(it):
                b = it.b
                if it.live(0):
                    copy_v(b, 0)
                    copy_v(b, 1)
                if it.live(1):
                    root(b + 1, stats1, mean_var1[:, :, 1], var_eps1[:, :], rstd1[:, :], stats1_done,
                         b * 4 + 8, var1_done, b + 2, rstd1_done)
                if it.live(0):
                    copy_v(b, 2)
                    copy_v(b, 3)
                if it.live(-1):
                    for c in range(CH):
                        root(b - 1, stats2, mean_var2[:, c:c + 1, 1], var_eps2[:, c:c + 1], rstd2[:, c:c + 1],
                             stats2_done, b * 4 + (2 * c - 2), var2_done, b * 2 + (c - 1), rstd2_done)

            run_iterations(pool, iteration)

        @block.scalar
        def _(act):
            def exps(batch, step, i):
                act.wait_ge(s2_ready, batch * UNITS + (4 * step + i + 1))
                if i == 0:
                    if counts(batch * STEPS + (step - 1)):
                        act.wait_ge(pv_done, batch * STEPS + (step - 1))
                nc.scalar.activation(probs[:, step % 2, i, :], s2_bank[i % 2][:, :], ACT.Exp,
                                     scale=SCALE).then_inc(exp_done, 1)

            def high_part(batch, name, hi, bias, chunk, n):
                act.wait_ge(qk_ready, batch * 4 + (n + 1))
                for q in (2 * chunk, 2 * chunk + 1):
                    if counts(batch * 96):
                        act.wait_ge(stack_in[q], batch * 96)
                nc.scalar.activation(hi[:, chunk, :], bank_of[name][:, :], ACT.Identity,
                                     bias=bias[:, chunk:chunk + 1]).then_inc(qk_hi_done, 1)

            def max_high(batch, q):
                act.wait_ge(max_turned, batch * 4 + (q + 1))
                if q:
                    act.wait_ge(max_rows_in[q - 1], batch * 32 + 32)
                else:
                    if counts(batch * 32):
                        act.wait_ge(max_rows_in[QUADS - 1], batch * 32)
                nc.scalar.copy(max_rows[:, 0, :], bank_of[f"max{q}"][0:4, :]).then_inc(max_hi_done, 1)

            def x_turn(batch, t):
                act.wait_ge(x_turned, batch * 2 + (t + 1))
                if counts(batch * 2):
                    act.wait_ge(hidden_ready, batch * 2)
                nc.scalar.copy(xn2_t[:, t, :, :].rearrange("p d r -> p (d r)"),
                               bank_of[f"x_turn{t}"][:, :]).then_inc(xn2_t_done, 1)

            def hidden_turn(batch, t):
                act.wait_ge(hidden_turned, batch * 2 + (t + 1))
                if counts(batch * 2):
                    act.wait_ge(y_ready, batch * 2)
                nc.scalar.copy(hidden_t[:, t, :, :].rearrange("p d r -> p (d r)"),
                               bank_of[f"hidden_turn{t}"][:, :]).then_inc(hidden_t_done, 1)

            def logits_out(batch):
                act.wait_ge(logits_ready, batch + 1)
                if counts(batch):
                    act.wait_ge(logit_turned, batch)
                nc.scalar.activation(logits_t[:, :], bank_of["logits"][0:E, 0:CH * P], ACT.Identity,
                                     bias=br_sb[:, 0:1]).then_inc(logits_t_done, 1)

            def logit_exp(batch):
                act.wait_ge(route_done, batch * ROUTE + 3)
                nc.scalar.activation(exp_logit[:, :, :], below_top[:, :, :], ACT.Exp).then_inc(exp_logit_done, 1)

            def iteration(it):
                b = it.b
                for s in range(STEPS):
                    for i in range(5):
                        if (s, i) == (0, 4) and it.live(-2):
                            hidden_turn(b - 2, 0)
                        if (s, i) == (1, 2) and it.live(-1):
                            max_high(b - 1, 3)
                        if (s, i) == (1, 4) and it.live(-2):
                            hidden_turn(b - 2, 1)
                        if s in (5, 9, 13) and i == 2 and it.live(0):
                            max_high(b, (s - 5) // 4)
                        if (s, i) == (6, 4) and it.live(1):
                            high_part(b + 1, "q0", q_hi, bq_sb, 0, 0)
                        if (s, i) == (7, 4) and it.live(1):
                            high_part(b + 1, "k0", k_hi, bk_sb, 0, 1)
                        if (s, i) == (9, 4) and it.live(1):
                            high_part(b + 1, "q1", q_hi, bq_sb, 1, 2)
                        if (s, i) == (11, 4) and it.live(1):
                            high_part(b + 1, "k1", k_hi, bk_sb, 1, 3)
                        if s in (12, 13) and i == 4 and it.live(-1):
                            x_turn(b - 1, s - 12)
                        if (s, i) == (14, 4) and it.live(-1):
                            logits_out(b - 1)
                        if (s, i) == (15, 4) and it.live(-1):
                            logit_exp(b - 1)
                        if i < 4 and s < LAG and it.live(-1):
                            exps(b - 1, s + LAG, i)
                        if i < 4 and s >= LAG and it.live(0):
                            exps(b, s - LAG, i)

            act.wait_ge(weights_in, all_weights)
            run_iterations(act, iteration)

        @block.vector
        def _(dve):
            nc.vector.memset(q_stack[0:SPLIT_ROWS, :, :].bitcast(F32), 0.0).then_inc(pad_set, 1)
            nc.vector.memset(k_stack[0:SPLIT_ROWS, :, :].bitcast(F32), 0.0).then_inc(pad_set, 1)

            def row_max(batch, q, piece, i):
                dve.wait_ge(s1_ready, batch * UNITS + (16 * q + 4 * piece + i + 1))
                nc.vector.tensor_reduce(neg_max[:, q, piece, i:i + 1], s1_bank[i % 2][:, :], X_AXIS, ALU.max,
                                        negate=True).then_inc(max_done, 1)

            def max_low(batch, q):
                dve.wait_ge(max_hi_done, batch * 4 + (q + 1))
                nc.vector.tensor_tensor(max_rows[:, 1, :], bank_of[f"max{q}"][0:4, :], max_rows[:, 0, :],
                                        ALU.subtract).then_inc(max_lo_done, 1)

            def low_part(batch, name, hi, lo, bias, chunk, n):
                dve.wait_ge(qk_hi_done, batch * 4 + (n + 1))
                nc.vector.scalar_tensor_tensor(
                    out=lo[:, chunk, :], in0=bank_of[name][:, :], scalar=bias[:, chunk:chunk + 1],
                    in1=hi[:, chunk, :], op0=ALU.add, op1=ALU.subtract).then_inc(qk_lo_done, 1)

            def turn_quad(batch, q):
                first = batch * NORM + QUAD_NORM[q]
                if counts(first):
                    dve.wait_ge(norm_done, first)
                dve.wait_ge(pv_done, batch * STEPS + (4 * q + 4))
                nc.vector.transpose(turned[:, :, :].rearrange("p n k -> p (n k)"),
                                    pv_bank[:, :]).then_inc(norm_done, 1)

            def normalise(batch, q):
                first = batch * NORM + QUAD_NORM[q]
                dve.wait_ge(norm_done, first + 1)
                nc.vector.reciprocal(inv_sum[:, :, :], turned[:, :, KC:KC + 1]).then_inc(norm_done, 1)
                dve.wait_ge(norm_done, first + 2)
                half = slice(KC * (q % 2), KC * (q % 2) + KC)
                nc.vector.tensor_tensor(normed[:, :, half], turned[:, :, 0:KC],
                                        inv_sum[:, :, :].to_broadcast([P, BLOCKS, KC]),
                                        ALU.mult).then_inc(norm_done, 1)
                if q % 2:
                    dve.wait_ge(norm_done, first + 3)
                    if counts(batch * 2):
                        dve.wait_ge(out_ready, batch * 2)
                    nc.vector.transpose(heads_out[:, q // 2, :],
                                        normed[:, :, :].rearrange("p n k -> p (n k)")).then_inc(norm_done, 1)

            def statistics(batch, c, source, stats, mean_var, done):
                nc.vector.bn_stats(stats[:, c, :], source[:, c, :]).then_inc(done, 1)
                dve.wait_ge(done, batch * 4 + (2 * c + 1))
                stand_alone(dve, passed)
                nc.vector.bn_aggr(mean_var[:, c, :], stats[:, c, :]).then_inc(done, 1)

            def scale_rows(c, to, source, mean_var, rstd, done):
                nc.vector.tensor_scalar(to[:, c, :], source[:, c, :], mean_var[:, c, 0:1], rstd[:, c:c + 1],
                                        ALU.subtract, ALU.mult).then_inc(done, 1)

            def statistics1(batch):
                dve.wait_ge(x_in, batch * 16 + 16)
                for c in range(CH):
                    statistics(batch, c, x_raw, stats1, mean_var1, stats1_done)

            def layernorm1(batch):
                dve.wait_ge(rstd1_done, batch + 1)
                if counts(batch * 4 - 1):
                    dve.wait_ge(qk_ready, batch * 4 - 1)
                for c in range(CH):
                    scale_rows(c, xn, x_raw, mean_var1, rstd1, xn_done)

            def v_add(batch, half):
                dve.wait_ge(v_ready, batch * 2 + (half + 1))
                if counts(batch * 4):
                    dve.wait_ge(v_ones_done, batch * 4)
                nc.vector.tensor_tensor(
                    v_plain[:, 2 * half:2 * half + 2, :],
                    bank_of[f"v{half}"][:, :].rearrange("p (s c) -> p s c", s=2),
                    bv_sb[:, :].unsqueeze(1).to_broadcast([P, 2, C]), ALU.add).then_inc(v_plain_done, 1)

            def residual(batch, c):
                dve.wait_ge(out_ready, batch * 2 + (c + 1))
                dve.wait_ge(x_again_in, batch * 16 + 16)
                nc.vector.scalar_tensor_tensor(
                    out=x2[:, c, :], in0=bank_of[f"out{c}"][:, :], scalar=bo_sb[:, c:c + 1],
                    in1=x_again[:, c, :], op0=ALU.add, op1=ALU.add).then_inc(x2_done, 1)
                dve.wait_ge(x2_done, batch * 2 + (c + 1))
                statistics(batch, c, x2, stats2, mean_var2, stats2_done)

            def layernorm2(batch, c):
                dve.wait_ge(rstd2_done, batch * 2 + (c + 1))
                if counts(batch * 2):
                    dve.wait_ge(x_turned, batch * 2)
                scale_rows(c, xn2, x2, mean_var2, rstd2, xn2_done)

            def route_start(batch):
                n = batch * ROUTE
                wide = [P, CH, E]
                dve.wait_ge(logit_turned, batch + 1)
                nc.vector.tensor_copy(logit[:, :, :],
                                      bank_of["logit_turn"][:, 0:CH * E].rearrange("p (t e) -> p t e", t=CH)
                                      ).then_inc(route_done, 1)
                dve.wait_ge(route_done, n + 1)
                nc.vector.tensor_reduce(top[:, :, :], logit[:, :, :], X_AXIS, ALU.max).then_inc(route_done, 1)
                dve.wait_ge(route_done, n + 2)
                nc.vector.tensor_tensor(below_top[:, :, :], logit[:, :, :], top[:, :, :].to_broadcast(wide),
                                        ALU.subtract).then_inc(route_done, 1)
                nc.vector.tensor_tensor(is_top[:, :, :], logit[:, :, :], top[:, :, :].to_broadcast(wide),
                                        ALU.is_equal).then_inc(route_done, 1)

            def route_end(batch):
                n = batch * ROUTE
                wide = [P, CH, E]
                dve.wait_ge(route_done, n + 4)
                nc.vector.tensor_tensor(top_rank[:, :, :], is_top[:, :, :], rank[:, :, :],
                                        ALU.mult).then_inc(route_done, 1)
                dve.wait_ge(route_done, n + 5)
                nc.vector.tensor_reduce(best_rank[:, :, :], top_rank[:, :, :], X_AXIS,
                                        ALU.max).then_inc(route_done, 1)
                dve.wait_ge(route_done, n + 6)
                nc.vector.tensor_tensor(chosen[:, :, :], top_rank[:, :, :], best_rank[:, :, :].to_broadcast(wide),
                                        ALU.is_equal).then_inc(route_done, 1)
                dve.wait_ge(exp_logit_done, batch + 1)
                nc.vector.tensor_reduce(exp_sum[:, :, :], exp_logit[:, :, :], X_AXIS,
                                        ALU.add).then_inc(route_done, 1)
                dve.wait_ge(route_done, n + 8)
                nc.vector.reciprocal(weight[:, :, :], exp_sum[:, :, :]).then_inc(route_done, 1)
                dve.wait_ge(route_done, n + 9)
                nc.vector.scalar_tensor_tensor(
                    out=gate[:, :, :], in0=chosen[:, :, :], scalar=1.0 / R, in1=weight[:, :, :].to_broadcast(wide),
                    op0=ALU.mult, op1=ALU.mult).then_inc(route_done, 1)

            def gate_hidden(batch, t):
                dve.wait_ge(route_done, batch * ROUTE + ROUTE)
                dve.wait_ge(hidden_ready, batch * 2 + (t + 1))
                if counts(batch * 2):
                    dve.wait_ge(hidden_turned, batch * 2)
                nc.vector.tensor_tensor(
                    hidden[:, t, :].rearrange("p (e r) -> p e r", e=E),
                    bank_of[f"hidden{t}"][:, :].rearrange("p (e r) -> p e r", e=E),
                    gate[:, t, :].unsqueeze(2).to_broadcast([P, E, R]), ALU.mult).then_inc(hidden_done, 1)

            def result(batch, t):
                dve.wait_ge(y_ready, batch * 2 + (t + 1))
                if counts(batch * 16):
                    dve.wait_ge(out_stored[t], batch * 16)
                nc.vector.tensor_tensor(y_out[:, t, :], bank_of[f"y{t}"][:, :], x2[:, t, :],
                                        ALU.add).then_inc(y_done, 1)

            def iteration(it):
                b = it.b
                for s in range(STEPS):
                    for i in range(4):
                        if it.live(0):
                            row_max(b, s // PIECES, s % PIECES, i)
                        if (s, i) == (0, 0) and it.live(-2):
                            route_end(b - 2)
                        if (s, i) == (0, 1) and it.live(-2):
                            gate_hidden(b - 2, 0)
                        if (s, i) == (1, 0) and it.live(-1):
                            turn_quad(b - 1, 1)
                        if (s, i) == (1, 0) and it.live(-2):
                            gate_hidden(b - 2, 1)
                        if (s, i) == (1, 1) and it.live(-1):
                            normalise(b - 1, 1)
                        if (s, i) == (1, 3) and it.live(-1):
                            max_low(b - 1, 3)
                        if (s, i) == (2, 3) and it.live(1):
                            statistics1(b + 1)
                        if (s, i) == (3, 2) and it.live(-2):
                            result(b - 2, 0)
                        if (s, i) == (4, 2) and it.live(1):
                            layernorm1(b + 1)
                        if (s, i) == (5, 0) and it.live(-1):
                            turn_quad(b - 1, 2)
                        if (s, i) == (5, 1) and it.live(-1):
                            normalise(b - 1, 2)
                        if s in (5, 9, 13) and i == 3 and it.live(0):
                            max_low(b, (s - 5) // 4)
                        if (s, i) == (5, 3) and it.live(-2):
                            result(b - 2, 1)
                        if (s, i) == (7, 1) and it.live(1):
                            low_part(b + 1, "q0", q_hi, q_lo, bq_sb, 0, 0)
                        if (s, i) == (8, 1) and it.live(1):
                            low_part(b + 1, "k0", k_hi, k_lo, bk_sb, 0, 1)
                        if (s, i) == (9, 0) and it.live(-1):
                            turn_quad(b - 1, 3)
                        if (s, i) == (9, 1) and it.live(-1):
                            normalise(b - 1, 3)
                        if (s, i) == (9, 2) and it.live(1):
                            v_add(b + 1, 0)
                        if (s, i) == (10, 1) and it.live(1):
                            low_part(b + 1, "q1", q_hi, q_lo, bq_sb, 1, 2)
                        if (s, i) == (10, 3) and it.live(-1):
                            residual(b - 1, 0)
                        if (s, i) == (11, 1) and it.live(-1):
                            residual(b - 1, 1)
                        if (s, i) == (11, 3) and it.live(-1):
                            layernorm2(b - 1, 0)
                        if (s, i) == (12, 0) and it.live(1):
                            low_part(b + 1, "k1", k_hi, k_lo, bk_sb, 1, 3)
                        if (s, i) == (12, 1) and it.live(-1):
                            layernorm2(b - 1, 1)
                        if (s, i) == (12, 2) and it.live(1):
                            v_add(b + 1, 1)
                        if (s, i) == (13, 0) and it.live(0):
                            turn_quad(b, 0)
                        if (s, i) == (13, 1) and it.live(0):
                            normalise(b, 0)
                        if (s, i) == (15, 2) and it.live(-1):
                            route_start(b - 1)

            dve.wait_ge(weights_in, all_weights)
            dve.wait_ge(ident_set, 6)
            run_iterations(dve, iteration)

        @block.tensor
        def _(pe):
            def scores_for_max(batch, s, i):
                q, head, rows = s // PIECES, 4 * (s // PIECES) + i, slice(P * (s % PIECES), P * (s % PIECES) + P)
                if s % PIECES == 0 and i == 0:
                    pe.wait_ge(stack_in[q], batch * 96 + 96)
                if counts(batch * UNITS + (4 * s + i - 1)):
                    pe.wait_ge(max_done, batch * UNITS + (4 * s + i - 1))
                nc.tensor.matmul(s1_bank[i % 2][:, :], q_stack[0:SPLIT_ROWS, head, rows],
                                 k_stack[0:SPLIT_ROWS, head, :], start=True, stop=True).then_inc(s1_ready, 1)

            def scores_less_max(batch, s, i):
                q, head, rows = s // PIECES, 4 * (s // PIECES) + i, slice(P * (s % PIECES), P * (s % PIECES) + P)
                if s % PIECES == 0 and i == 0:
                    pe.wait_ge(max_rows_in[q], batch * 32 + 32)
                if counts(batch * UNITS + (4 * s + i - 1)):
                    pe.wait_ge(exp_done, batch * UNITS + (4 * s + i - 1))
                nc.tensor.matmul(s2_bank[i % 2][:, :], k_stack[0:FULL_ROWS, head, rows],
                                 q_stack[0:FULL_ROWS, head, :], start=True, stop=True).then_inc(s2_ready, 1)

            def probs_times_v(batch, s):
                q, piece = s // PIECES, s % PIECES
                if piece == 0:
                    pe.wait_ge(v_ones_done, batch * 4 + (q + 1))
                    last = QUAD_NORM[q - 1] if q else QUAD_NORM[QUADS - 1] - NORM
                    if counts(batch * NORM + (last + 1)):
                        pe.wait_ge(norm_done, batch * NORM + (last + 1))
                pe.wait_ge(exp_done, batch * UNITS + (4 * s + 4))
                for i in range(4):
                    last = nc.tensor.matmul(pv_bank[32 * i:32 * i + 32, :], v_ones[:, q, piece, i, :],
                                            probs[:, s % 2, i, :], start=piece == 0, stop=piece == PIECES - 1)
                last.then_inc(pv_done, 1)

            def project(it, name, weights, source, c, kc):
                return nc.tensor.matmul(bank_of[name][:, :], weights[:, kc, P * c:P * c + P], source[:, kc, :],
                                        start=kc == 0, stop=kc == CH - 1)

            def query(it, c, kc):
                b = it.b
                if kc == 0:
                    if c == 1:
                        pe.wait_ge(qk_lo_done, b * 4 + 5)
                    elif it.live(-2):
                        pe.wait_ge(y_done, b * 2 - 3)
                    elif it.live(0):
                        pe.wait_ge(qk_lo_done, b * 4 + 4)
                    pe.wait_ge(xn_done, b * 2 + 4)
                last = project(it, f"q{c}", wq_sb, xn, c, kc)
                if kc == CH - 1:
                    last.then_inc(qk_ready, 1)

            def key(it, c, kc):
                b = it.b
                if kc == 0:
                    if c == 1:
                        pe.wait_ge(qk_lo_done, b * 4 + 7)
                    elif it.live(-2):
                        pe.wait_ge(y_done, b * 2 - 2)
                    elif it.live(-1):
                        pe.wait_ge(max_lo_done, b * 4)
                    elif it.live(0):
                        pe.wait_ge(qk_lo_done, b * 4 + 2)
                    pe.wait_ge(ctx_in_sem, b * 16 + 32)
                last = project(it, f"k{c}", wk_sb, ctx_sb, c, kc)
                if kc == CH - 1:
                    last.then_inc(qk_ready, 1)

            def value(it, half, n):
                b = it.b
                if n == 0:
                    if half == 0 and it.live(0):
                        pe.wait_ge(max_lo_done, b * 4 + 1)
                    elif half == 1 and it.live(-1):
                        pe.wait_ge(x2_done, b * 2 - 1)
                    elif half == 1:
                        pe.wait_ge(v_plain_done, b * 2 + 3)
                rows = slice(P * (2 * half + n), P * (2 * half + n) + P)
                for kc in range(CH):
                    last = nc.tensor.matmul(bank_of[f"v{half}"][:, C * n:C * n + C], ctx_sb[:, kc, rows],
                                            wv_sb[:, kc, :], start=kc == 0, stop=kc == CH - 1)
                if n == 1:
                    last.then_inc(v_ready, 1)

            def output(it, c, kc):
                b = it.b
                if kc == 0:
                    if c == 0 and it.live(1):
                        pe.wait_ge(v_plain_done, b * 2 + 3)
                    elif c == 1 and it.live(0):
                        pe.wait_ge(max_lo_done, b * 4 + 2)
                    pe.wait_ge(norm_done, b * NORM)
                last = project(it, f"out{c}", wo_sb, heads_out, c, kc)
                if kc == CH - 1:
                    last.then_inc(out_ready, 1)

            def turn_max(it, off, q):
                b = it.b
                if q == 3 and it.live(-2):
                    pe.wait_ge(route_done, b * ROUTE + (1 - 2 * ROUTE))
                elif q == 3:
                    pe.wait_ge(max_lo_done, b * 4 - 2)
                elif q == 0 and it.live(-2):
                    pe.wait_ge(hidden_t_done, b * 2 - 2)
                elif q == 0 and it.live(-1):
                    pe.wait_ge(max_lo_done, b * 4 - 1)
                elif q == 0:
                    pe.wait_ge(v_plain_done, b * 2 + 2)
                elif q == 1 and it.live(1):
                    pe.wait_ge(qk_lo_done, b * 4 + 6)
                elif q == 1:
                    pe.wait_ge(y_done, b * 2 - 2)
                elif it.live(1):
                    pe.wait_ge(v_plain_done, b * 2 + 4)
                else:
                    pe.wait_ge(x2_done, b * 2 - 1)
                pe.wait_ge(max_done, (b + off) * UNITS + (16 * q + 16))
                for piece in range(PIECES):
                    last = nc.tensor.matmul(bank_of[f"max{q}"][0:4, P * piece:P * piece + P],
                                            neg_max[:, q, piece, :], ident[:, :], start=True, stop=True)
                last.then_inc(max_turned, 1)

            def turn_x(batch, t):
                if t == 0:
                    pe.wait_ge(x2_done, batch * 2 + 2)
                else:
                    pe.wait_ge(xn2_t_done, batch * 2 + 1)
                pe.wait_ge(xn2_done, batch * 2 + (t + 1))
                for d in range(DCH):
                    last = nc.tensor.transpose(bank_of[f"x_turn{t}"][:, P * d:P * d + P],
                                               xn2[:, t, P * d:P * d + P], ident[:, :])
                last.then_inc(x_turned, 1)

            def router(it, half):
                if half == 0:
                    if it.live(1):
                        pe.wait_ge(qk_lo_done, it.b * 4 + 8)
                    pe.wait_ge(xn2_t_done, it.b * 2)
                for d in (2 * half, 2 * half + 1):
                    last = nc.tensor.matmul(bank_of["logits"][0:E, 0:CH * P], wr_sb[:, d, :], xn2_t[:, :, d, :],
                                            start=d == 0, stop=d == DCH - 1)
                if half == 1:
                    last.then_inc(logits_ready, 1)

            def turn_logits(batch):
                pe.wait_ge(logits_t_done, batch + 1)
                stand_alone(pe, passed)
                for t in range(CH):
                    last = nc.tensor.transpose(bank_of["logit_turn"][:, E * t:E * t + E],
                                               logits_t[:, P * t:P * t + P], ident[0:E, 0:E])
                last.then_inc(logit_turned, 1)

            def expert_in(it, batch, t, d):
                if d == 0:
                    if t == 0 and it.live(0):
                        pe.wait_ge(max_lo_done, it.b * 4 + 3)
                    pe.wait_ge(xn2_t_done, batch * 2 + (t + 1))
                last = nc.tensor.matmul(bank_of[f"hidden{t}"][:, :], xn2_t[:, t, d, :], a_sb[:, d, :],
                                        start=d == 0, stop=d == DCH - 1)
                if d == DCH - 1:
                    last.then_inc(hidden_ready, 1)

            def turn_hidden(batch, t):
                if t == 1:
                    pe.wait_ge(hidden_t_done, batch * 2 + 1)
                pe.wait_ge(hidden_done, batch * 2 + (t + 1))
                for d in range(DCH):
                    last = nc.tensor.transpose(bank_of[f"hidden_turn{t}"][:, P * d:P * d + P],
                                               hidden[:, t, P * d:P * d + P], ident[:, :])
                last.then_inc(hidden_turned, 1)

            def expert_out(it, batch, t, d):
                if d == 0:
                    if t == 0:
                        pe.wait_ge(hidden_done, batch * 2 + 2)
                    elif it.live(-1):
                        pe.wait_ge(max_lo_done, it.b * 4)
                    pe.wait_ge(hidden_t_done, batch * 2 + (t + 1))
                last = nc.tensor.matmul(bank_of[f"y{t}"][:, :], hidden_t[:, t, d, :], b_sb[:, d, :],
                                        start=d == 0, stop=d == DCH - 1)
                if d == DCH - 1:
                    last.then_inc(y_ready, 1)

            def beside(it, s, i):
                b = it.b
                if it.live(-2):
                    if s == 0 and i < 3:
                        expert_in(it, b - 2, 1, i + 1)
                    if (s, i) == (0, 3):
                        turn_hidden(b - 2, 0)
                if it.live(-1) and (s, i) == (1, 0):
                    turn_max(it, -1, 3)
                if it.live(-2):
                    if (s, i) == (1, 3):
                        turn_hidden(b - 2, 1)
                    if (s, i) in FIRST_TILE_OUT:
                        expert_out(it, b - 2, 0, FIRST_TILE_OUT.index((s, i)))
                    if (s, i) in SECOND_TILE_OUT:
                        expert_out(it, b - 2, 1, SECOND_TILE_OUT.index((s, i)))
                if it.live(0) and s in (5, 9, 13) and i == 0:
                    turn_max(it, 0, (s - 5) // 4)
                if it.live(1):
                    if s == 6 and i in (0, 2):
                        query(it, 0, i // 2)
                    if s == 7 and i in (0, 2):
                        key(it, 0, i // 2)
                    if s == 8 and i in (1, 3):
                        value(it, 0, i // 2)
                    if s == 9 and i in (1, 2):
                        query(it, 1, i - 1)
                if it.live(-1):
                    if s == 10 and i > 0:
                        output(it, (i - 1) // 2, (i - 1) % 2)
                    if (s, i) == (11, 0):
                        output(it, 1, 1)
                if it.live(1):
                    if s == 11 and i in (1, 2):
                        key(it, 1, i - 1)
                    if s == 12 and i < 2:
                        value(it, 1, i)
                if it.live(-1):
                    if s in (12, 13) and i == 2:
                        turn_x(b - 1, s - 12)
                    if s == 14 and i in (0, 3):
                        expert_in(it, b - 1, 0, i // 3)
                    if s == 14 and i in (1, 2):
                        router(it, i - 1)
                    if s == 15 and i in (0, 2):
                        expert_in(it, b - 1, 0, 2 + i // 2)
                    if (s, i) == (15, 1):
                        turn_logits(b - 1)
                    if (s, i) == (15, 3):
                        expert_in(it, b - 1, 1, 0)

            def iteration(it):
                b = it.b
                for s in range(STEPS):
                    for i in range(4):
                        if it.live(0):
                            scores_for_max(b, s, i)
                        if s < LAG and it.live(-1):
                            scores_less_max(b - 1, s + LAG, i)
                        if s >= LAG and it.live(0):
                            scores_less_max(b, s - LAG, i)
                        if i == 2:
                            if s <= LAG and it.live(-1):
                                probs_times_v(b - 1, s + LAG - 1)
                            if s > LAG and it.live(0):
                                probs_times_v(b, s - LAG - 1)
                        beside(it, s, i)

            pe.wait_ge(weights_in, all_weights)
            pe.wait_ge(ident_set, 6)
            run_iterations(pe, iteration)


def kernel(**inputs):
    import numpy as np
    import concourse.bacc as bacc
    from concourse.bass_utils import run_bass_kernel_spmd

    a = {name: np.asarray(value) for name, value in inputs.items()}
    x, ctx = a["x"], a["ctx_2048"]

    def columns(w):
        return w.reshape(w.shape[0], -1, P).transpose(2, 1, 0)

    def by_quad(w):
        return w.reshape(QUADS, 4, KC, -1).transpose(0, 2, 1, 3).reshape(HEADS * KC, -1)

    def chunks(v):
        return v.reshape(CH, P).transpose(1, 0)

    wo = a["L0_xattn_Wo"].reshape(C, CH, 2, 4, KC).transpose(3, 2, 4, 1, 0).reshape(P, CH, C)
    expert_b = a["L0_ffn_B"].transpose(0, 2, 1).reshape(DCH, P, D).transpose(1, 0, 2)
    arrays = {
        "x": x, "ctx_in": ctx,
        "wq_t": columns(by_quad(a["L0_xattn_Wq"])), "wk_t": columns(by_quad(a["L0_xattn_Wk"])),
        "wv_t": columns(a["L0_xattn_Wv"]), "wo_t": wo,
        "bq": chunks(by_quad(a["L0_xattn_bq"])), "bk": chunks(by_quad(a["L0_xattn_bk"])),
        "bv": a["L0_xattn_bv"], "bo": chunks(a["L0_xattn_bo"]),
        "a_t": columns(a["L0_ffn_A"].reshape(E * R, D)), "b_t": expert_b,
        "wr_t": columns(a["L0_ffn_Wr"]), "br": a["L0_ffn_br"].reshape(E, 1),
    }
    arrays = {f"{name}_dram": np.ascontiguousarray(value) for name, value in arrays.items()}
    nc = bacc.Bacc("TRN2", target_bir_lowering=False, num_devices=1)
    args = [nc.dram_tensor(name, v.shape, mybir.dt.from_np(v.dtype), kind="ExternalInput").ap()
            for name, v in arrays.items()]
    args.append(nc.dram_tensor("out_dram", (BATCHES, C, T), F32, kind="ExternalOutput").ap())
    xattn_experts(nc, *args)
    r = run_bass_kernel_spmd(nc, [arrays], core_ids=[0])
    return r.results[0]["out_dram"]
```

```python
from contextlib import ExitStack

import concourse.bass as bass
from concourse import mybir

F32 = mybir.dt.float32
F32R = mybir.dt.float32r
ALU = mybir.AluOpType
ACT = mybir.ActivationFunctionType
X_AXIS = mybir.AxisListType.X

P = 128
BATCHES, C, T = 16, 256, 512
HEADS, KC = 16, 16
SCALE = float(KC) ** -0.5
E, R, D = 8, 64, 512
EPS = 1e-5

CH = C // P
DCH = D // P
QUADS = HEADS // 4
PIECES = T // P
STEPS = QUADS * PIECES
LAG = STEPS // 2
UNITS = 4 * STEPS
SPLIT_ROWS = 96
FULL_ROWS = SPLIT_ROWS + 2
NORM = 14
QUAD_NORM = [0, 3, 7, 10]
ROUTE = 10
BLOCKS = T // 32
V_ROW = 3 * (KC + 1) + 32

BANK_TURNS = [
    ("hidden1", "y0", "q0", "q1", "k1", "logits"),
    ("hidden_turn0", "hidden_turn1", "max0", "v0", "out0", "max2", "v1", "hidden0"),
    ("max3", "y1", "k0", "max1", "out1", "x_turn0", "x_turn1", "logit_turn"),
]
FIRST_TILE_OUT = [(1, 1), (2, 0), (2, 1), (2, 3), (3, 0), (3, 1)]
SECOND_TILE_OUT = [(3, 3), (4, 0), (4, 1), (4, 3), (5, 0), (5, 1)]
Q0, K0, V0 = [(5, 3), (6, 0), (6, 1)], [(6, 3), (7, 0), (7, 1)], [(7, 3), (8, 0), (8, 1)]
Q1, K1, V1 = [(8, 3), (9, 0), (9, 1)], [(11, 1), (11, 3), (12, 1)], [(13, 0), (13, 1)]
TURN_MAX = [(5, 0), (9, 0), (12, 0)]
OUTPUT = [(9, 3), (10, 1), (10, 3), (11, 0)]
FIRST_FULL, LAST_FULL = 3, BATCHES - 3


class Iteration:

    def __init__(self, b, looped=False):
        self.b, self.looped = b, looped

    def live(self, offset):
        return self.looped or 0 <= self.b + offset < BATCHES


def counts(n):
    return not isinstance(n, int) or n > 0


def stand_alone(eng, sem):
    eng.sem_inc(sem, 1)


def run_iterations(eng, body):
    for b in range(-1, FIRST_FULL):
        body(Iteration(b))
    with eng.Fori(FIRST_FULL, LAST_FULL + 1) as b:
        body(Iteration(b, looped=True))
    for b in range(LAST_FULL + 1, BATCHES + 2):
        body(Iteration(b))


def xattn_experts(nc, x, ctx_in, wq_t, wk_t, wv_t, wo_t, bq, bk, bv, bo, a_t, b_t, wr_t, br, out):
    with ExitStack() as stack:
        def sb(name, shape, dt=F32):
            return stack.enter_context(nc.sbuf_tensor(name, shape, dt))

        def bank(name):
            return stack.enter_context(nc.psum_tensor(name, [P, 512], F32))

        def sem(name):
            return stack.enter_context(nc.semaphore(name))

        def split(name, shape):
            return sb(f"{name}_hi", shape, F32R), sb(f"{name}_lo", shape, F32R)

        wq_parts = split("wq", [P, CH, C])
        wk_parts = split("wk", [P, CH, C])
        wv_parts = split("wv", [P, CH, C])
        wo_sb = sb("wo_sb", [P, CH, C])
        bq_sb = sb("bq_sb", [P, CH])
        bk_sb = sb("bk_sb", [P, CH])
        bv_sb = sb("bv_sb", [P, C])
        bo_sb = sb("bo_sb", [P, CH])
        a_parts = split("a", [P, DCH, E * R])
        b_parts = split("b", [P, DCH, D])
        wr_parts = split("wr", [P, DCH, E])
        br_sb = sb("br_sb", [E, 1])
        ident = sb("ident", [P, P])
        rank = sb("rank", [P, CH, E])
        minus_half = sb("minus_half", [P, CH])

        ctx_raw = sb("ctx_raw", [P, CH, T])
        ctx_parts = split("ctx", [P, CH, T])
        xn = sb("xn", [P, CH, T])
        xn_parts = split("xn", [P, CH, T])
        q_hi = sb("q_hi", [P, CH, T], F32R)
        q_lo = sb("q_lo", [P, CH, T], F32R)
        k_hi = sb("k_hi", [P, CH, T], F32R)
        k_lo = sb("k_lo", [P, CH, T], F32R)
        q_stack = sb("q_stack", [P, HEADS, T], F32R)
        k_stack = sb("k_stack", [P, HEADS, T], F32R)
        neg_max = sb("neg_max", [P, QUADS, 4, PIECES])
        max_rows = sb("max_rows", [4 * PIECES, 2, P], F32R)
        probs = sb("probs", [P, 2, 4, T])
        v_plain = sb("v_plain", [P, PIECES, C])
        v_ones = sb("v_ones", [P, QUADS, PIECES, V_ROW])
        turned = sb("turned", [P, BLOCKS, 32])
        inv_sum = sb("inv_sum", [P, BLOCKS, 1])
        normed = sb("normed", [P, BLOCKS, 32])
        heads_out = sb("heads_out", [P, CH, T])

        x2 = sb("x2", [P, CH, T])
        xn2 = hidden = y_out = sb("row_tiles", [P, CH, T])
        xn2_t_parts = hidden_t_parts = split("turned_rows", [P, CH, DCH, P])
        stats1 = sb("stats1", [P, CH, 6])
        mean_var1 = sb("mean_var1", [P, CH, 2])
        var_eps1 = sb("var_eps1", [P, CH])
        rstd1 = sb("rstd1", [P, CH])
        stats2 = sb("stats2", [P, CH, 6])
        mean_var2 = sb("mean_var2", [P, CH, 2])
        var_eps2 = sb("var_eps2", [P, CH])
        rstd2 = sb("rstd2", [P, CH])
        logits_t = sb("logits_t", [E, CH * P])
        logit = sb("logit", [P, CH, E])
        top = sb("top", [P, CH, 1])
        below_top = sb("below_top", [P, CH, E])
        exp_logit = sb("exp_logit", [P, CH, E])
        exp_sum = sb("exp_sum", [P, CH, 1])
        weight = sb("weight", [P, CH, 1])
        is_top = sb("is_top", [P, CH, E])
        top_rank = sb("top_rank", [P, CH, E])
        best_rank = sb("best_rank", [P, CH, 1])
        chosen = sb("chosen", [P, CH, E])
        gate = sb("gate", [P, CH, E])

        s1_bank = [bank(f"s1_bank{i}") for i in range(2)]
        s2_bank = [bank(f"s2_bank{i}") for i in range(2)]
        pv_bank = bank("pv_bank")
        bank_of = {}
        for k, turns in enumerate(BANK_TURNS):
            bank_of.update(dict.fromkeys(turns, bank(f"side_bank{k}")))

        first_weights_in = sem("first_weights_in")
        later_weights_in = sem("later_weights_in")
        first_zeros_set = sem("first_zeros_set")
        pads_set = sem("pads_set")
        ident_set = sem("ident_set")
        passed = sem("passed")
        x_in = sem("x_in")
        ctx_in_sem = sem("ctx_in_sem")
        x_again_in = sem("x_again_in")
        weights_hi_done = sem("weights_hi_done")
        weights_lo_done = sem("weights_lo_done")
        ctx_hi_done = sem("ctx_hi_done")
        ctx_lo_done = sem("ctx_lo_done")
        xn_hi_done = sem("xn_hi_done")
        xn_lo_done = sem("xn_lo_done")
        stack_in = [sem(f"stack_in{q}") for q in range(QUADS)]
        max_rows_in = [sem(f"max_rows_in{q}") for q in range(QUADS)]
        out_stored = [sem(f"out_stored{t}") for t in range(CH)]
        s1_ready = sem("s1_ready")
        max_done = sem("max_done")
        s2_ready = sem("s2_ready")
        exp_done = sem("exp_done")
        pv_done = sem("pv_done")
        norm_done = sem("norm_done")
        qk_ready = sem("qk_ready")
        qk_hi_done = sem("qk_hi_done")
        qk_lo_done = sem("qk_lo_done")
        v_ready = sem("v_ready")
        v_plain_done = sem("v_plain_done")
        v_ones_done = sem("v_ones_done")
        max_turned = sem("max_turned")
        max_hi_done = sem("max_hi_done")
        max_lo_done = sem("max_lo_done")
        out_ready = sem("out_ready")
        x2_done = sem("x2_done")
        x_turned = sem("x_turned")
        xn2_t_hi_done = sem("xn2_t_hi_done")
        xn2_t_lo_done = sem("xn2_t_lo_done")
        logits_ready = sem("logits_ready")
        logits_t_done = sem("logits_t_done")
        logit_turned = sem("logit_turned")
        hidden_ready = sem("hidden_ready")
        hidden_done = sem("hidden_done")
        hidden_turned = sem("hidden_turned")
        hidden_t_hi_done = sem("hidden_t_hi_done")
        hidden_t_lo_done = sem("hidden_t_lo_done")
        y_ready = sem("y_ready")
        y_done = sem("y_done")
        stats1_done = sem("stats1_done")
        var1_done = sem("var1_done")
        rstd1_done = sem("rstd1_done")
        xn_done = sem("xn_done")
        stats2_done = sem("stats2_done")
        var2_done = sem("var2_done")
        rstd2_done = sem("rstd2_done")
        xn2_done = sem("xn2_done")
        route_done = sem("route_done")
        exp_logit_done = sem("exp_logit_done")

        def quad_v(q):
            return v_ones[:, q, :, 0:4 * (KC + 1)].rearrange("p s (i k) -> p s i k", k=KC + 1)

        x_view = x.rearrange("b (c p) t -> b p c t", p=P)
        ctx_view = ctx_in.rearrange("b (c p) t -> b p c t", p=P)
        out_view = out.rearrange("b (c p) t -> b p c t", p=P)

        first_splits = [(wq_parts, x2[:, 0, :].rearrange("p (c o) -> p c o", c=CH)),
                        (wk_parts, x2[:, 1, :].rearrange("p (c o) -> p c o", c=CH)),
                        (wv_parts, xn2[:, 0, :].rearrange("p (c o) -> p c o", c=CH))]
        later_splits = [(wr_parts, xn2[:, 1, 0:DCH * E].rearrange("p (d e) -> p d e", d=DCH)),
                        (a_parts, probs[:, 0, :, :]), (b_parts, probs[:, 1, :, :])]
        (_, wq_raw), (_, wk_raw), (_, wv_raw) = first_splits
        (_, wr_raw), (_, a_raw), (_, b_raw) = later_splits
        first_loads = [(wq_raw, wq_t), (bq_sb[:, :], bq), (wk_raw, wk_t), (bk_sb[:, :], bk), (wv_raw, wv_t),
                       (bv_sb[:, :], bv.partition_broadcast(P))]
        later_loads = [(wo_sb[:, :, :], wo_t), (bo_sb[:, :], bo), (wr_raw, wr_t), (br_sb[:, :], br),
                       (a_raw, a_t), (b_raw, b_t)]

        block = stack.enter_context(nc.Block())

        @block.sync
        def _(sp):
            def load_x(b):
                sp.dma_start(xn[:, :, :], x_view[b, :, :, :]).then_inc(x_in, 16)

            def load_ctx(b):
                sp.dma_start(ctx_raw[:, :, :], ctx_view[b, :, :, :]).then_inc(ctx_in_sem, 16)

            def stack_quad(b, q):
                c = q // 2
                sp.wait_ge(qk_lo_done, b * 4 + (2 * c + 2))
                stand_alone(sp, passed)
                if counts(b * UNITS + (16 * q + 16 - UNITS)):
                    sp.wait_ge(s2_ready, b * UNITS + (16 * q + 16 - UNITS))
                else:
                    if q == 0:
                        sp.wait_ge(first_zeros_set, 2)
                    sp.wait_ge(pads_set, (1, 4, 7, 10)[q])
                rows = slice(64 * (q % 2), 64 * (q % 2) + 64)
                heads = slice(4 * q, 4 * q + 4)
                for to, parts in ((q_stack, (q_hi, q_hi, q_lo)), (k_stack, (k_hi, k_lo, k_hi))):
                    for n, part in enumerate(parts):
                        sp.dma_start(to[16 * n:16 * n + 16, heads, :].bitcast(F32),
                                     part[rows, c, :].bitcast(F32)).then_inc(stack_in[q], 16)

            def stack_max(b, q):
                sp.wait_ge(max_lo_done, b * 4 + (q + 1))
                for n in range(2):
                    row = SPLIT_ROWS + n
                    to = q_stack[row:row + 1, 4 * q:4 * q + 4, :].rearrange("o h (s t) -> o (h s) t", t=P)
                    sp.dma_start(to.bitcast(F32), max_rows[:, n, :].bitcast(F32)).then_inc(max_rows_in[q], 16)

            def store(b, t):
                sp.wait_ge(y_done, b * 2 + (t + 1))
                stand_alone(sp, passed)
                sp.dma_start(out_view[b, :, t, :], y_out[:, t, :]).then_inc(out_stored[t], 16)

            load_x(0)
            load_ctx(0)
            for to, src in first_loads:
                sp.dma_start(to, src).then_inc(first_weights_in, 16)
            for to, src in later_loads:
                sp.dma_start(to, src).then_inc(later_weights_in, 16)

            def iteration(it):
                b = it.b
                if it.live(0):
                    stack_quad(b, 1)
                if it.live(-1):
                    stack_max(b - 1, 3)
                if it.live(-2):
                    store(b - 2, 0)
                if it.live(0):
                    stack_quad(b, 2)
                if it.live(0):
                    stack_max(b, 0)
                if it.live(-2):
                    store(b - 2, 1)
                if not it.looped and b == 1:
                    sp.wait_ge(weights_lo_done, len(first_splits))
                if it.live(-1):
                    sp.dma_start(x2[:, :, :], x_view[b - 1, :, :, :]).then_inc(x_again_in, 16)
                if it.live(0):
                    stack_quad(b, 3)
                    stack_max(b, 1)
                if it.live(2):
                    sp.wait_ge(xn_lo_done, b * 2 + 4)
                    stand_alone(sp, passed)
                    load_x(b + 2)
                    sp.wait_ge(ctx_lo_done, b * 2 + 4)
                    stand_alone(sp, passed)
                    load_ctx(b + 2)
                if it.live(1):
                    stack_quad(b + 1, 0)
                if it.live(0):
                    stack_max(b, 2)

            run_iterations(sp, iteration)
            for t in range(CH):
                sp.wait_ge(out_stored[t], 16 * BATCHES)

        @block.gpsimd
        def _(pool):
            nc.gpsimd.memset(ident[:, :], 0.0).then_inc(ident_set, 1)
            nc.gpsimd.memset(v_ones[:, :, :, :], 0.0).then_inc(ident_set, 1)
            for e in range(E):
                last = nc.gpsimd.memset(rank[:, :, e:e + 1], float(E - e))
            last.then_inc(ident_set, 1)
            nc.gpsimd.memset(minus_half[:, :], -0.5).then_inc(ident_set, 1)
            pool.wait_ge(ident_set, 4)
            nc.gpsimd.affine_select(out=ident[:, :], in_=ident[:, :], compare_op=ALU.not_equal, fill=1.0, base=0,
                                    pattern=[[-1, P]], channel_multiplier=1).then_inc(ident_set, 1)
            for q in range(QUADS):
                last = nc.gpsimd.memset(quad_v(q)[:, :, :, KC:KC + 1], 1.0)
            last.then_inc(ident_set, 1)
            pool.wait_ge(ident_set, 6)

            def set_zeros(to, q):
                nc.gpsimd.memset(to[0:SPLIT_ROWS, 4 * q:4 * q + 4, :].bitcast(F32), 0.0).then_inc(pads_set, 1)

            def set_ones(q):
                nc.gpsimd.memset(k_stack[SPLIT_ROWS:FULL_ROWS, 4 * q:4 * q + 4, :].bitcast(F32),
                                 1.0).then_inc(pads_set, 1)

            def set_pads(q):
                n = (0, 2, 4, 7)[q]
                set_zeros(q_stack, q)
                pool.wait_ge(pads_set, n + 1)
                set_zeros(k_stack, q)
                pool.wait_ge(pads_set, n + 2)
                if q > 1:
                    set_ones(q)
                    pool.wait_ge(pads_set, n + 3)

            for q in (0, 1):
                set_ones(q)
                pool.wait_ge(pads_set, q + 1)

            def bias_v(b, q):
                pool.wait_ge(v_plain_done, b * 2 + 2)
                if counts(b * STEPS + (4 * q + 4 - STEPS)):
                    pool.wait_ge(pv_done, b * STEPS + (4 * q + 4 - STEPS))
                stand_alone(pool, passed)
                bias = bv_sb[:, 64 * q:64 * q + 64].rearrange("p (i k) -> p i k", k=KC)
                nc.gpsimd.tensor_tensor(
                    quad_v(q)[:, :, :, 0:KC], v_plain[:, :, 64 * q:64 * q + 64].rearrange("p s (i k) -> p s i k", k=KC),
                    bias.unsqueeze(1).to_broadcast([P, PIECES, 4, KC]), ALU.add).then_inc(v_ones_done, 1)

            def low_rest(raw, parts, c, need_sem, need, done):
                pool.wait_ge(need_sem, need)
                stand_alone(pool, passed)
                nc.gpsimd.tensor_tensor(parts[1][:, c, :], raw[:, c, :], parts[0][:, c, :],
                                        ALU.subtract).then_inc(done, 1)

            def split_ctx(batch):
                for c in range(CH):
                    low_rest(ctx_raw, ctx_parts, c, ctx_hi_done, batch * 2 + (c + 1), ctx_lo_done)

            def split_weights(splits, n):
                for (hi, lo), raw in splits:
                    pool.wait_ge(weights_hi_done, n + 1)
                    nc.gpsimd.tensor_tensor(lo[:, :, :], raw, hi[:, :, :], ALU.subtract).then_inc(weights_lo_done, 1)
                    n += 1

            def root(b, stats, mean_var, var_eps, rstd, stats_sem, need, var_sem, var_count, rstd_sem):
                pool.wait_ge(stats_sem, need)
                stand_alone(pool, passed)
                nc.gpsimd.tensor_scalar(var_eps, mean_var, EPS, None, ALU.add).then_inc(var_sem, 1)
                pool.wait_ge(var_sem, var_count)
                nc.gpsimd.tensor_tensor(rstd, var_eps, minus_half[:, 0:rstd.shape[1]],
                                        ALU.pow).then_inc(rstd_sem, 1)

            def first_iteration():
                set_pads(2)
                split_weights(later_splits[:2], len(first_splits))
                split_ctx(1)
                root1(1)
                split_weights(later_splits[2:], len(first_splits) + 2)
                bias_v(0, 0)
                for c in range(CH):
                    low_rest(xn, xn_parts, c, xn_hi_done, c + 3, xn_lo_done)
                bias_v(0, 1)
                pool.wait_ge(v_ones_done, 2)
                set_pads(3)
                bias_v(0, 2)
                bias_v(0, 3)

            def root1(batch):
                root(batch, stats1, mean_var1[:, :, 1], var_eps1[:, :], rstd1[:, :], stats1_done,
                     batch * 4 + 4, var1_done, batch + 1, rstd1_done)

            def iteration(it):
                b = it.b
                if not it.looped and b == 0:
                    first_iteration()
                    return
                if it.live(1):
                    root1(b + 1)
                if it.live(0):
                    bias_v(b, 0)
                    bias_v(b, 1)
                if it.live(0) and it.live(1):
                    split_ctx(b + 1)
                if not it.looped and b == -1:
                    pool.wait_ge(rstd1_done, 1)
                    split_weights(first_splits, 0)
                    pool.wait_ge(weights_lo_done, len(first_splits))
                    set_pads(1)
                if it.live(0) and it.live(1):
                    for c in range(CH):
                        low_rest(xn, xn_parts, c, xn_hi_done, b * 2 + (c + 3), xn_lo_done)
                if it.live(0):
                    bias_v(b, 2)
                    bias_v(b, 3)
                if it.live(-1):
                    for c in range(CH):
                        root(b - 1, stats2, mean_var2[:, c:c + 1, 1], var_eps2[:, c:c + 1], rstd2[:, c:c + 1],
                             stats2_done, b * 4 + (2 * c - 2), var2_done, b * 2 + (c - 1), rstd2_done)

            run_iterations(pool, iteration)

        @block.scalar
        def _(act):
            def exps(batch, step, i):
                act.wait_ge(s2_ready, batch * UNITS + (4 * step + i + 1))
                if i == 0:
                    if counts(batch * STEPS + (step - 1)):
                        act.wait_ge(pv_done, batch * STEPS + (step - 1))
                nc.scalar.activation(probs[:, step % 2, i, :], s2_bank[i % 2][:, :], ACT.Exp,
                                     scale=SCALE).then_inc(exp_done, 1)

            def high_part(batch, name, hi, bias, chunk, n):
                act.wait_ge(qk_ready, batch * 4 + (n + 1))
                for q in (2 * chunk, 2 * chunk + 1):
                    if counts(batch * 96):
                        act.wait_ge(stack_in[q], batch * 96)
                nc.scalar.activation(hi[:, chunk, :], bank_of[name][:, :], ACT.Identity,
                                     bias=bias[:, chunk:chunk + 1]).then_inc(qk_hi_done, 1)

            def v_out(batch, half):
                act.wait_ge(v_ready, batch * 2 + (half + 1))
                if counts(batch * 4):
                    act.wait_ge(v_ones_done, batch * 4)
                nc.scalar.copy(v_plain[:, 2 * half:2 * half + 2, :].rearrange("p s c -> p (s c)"),
                               bank_of[f"v{half}"][:, :]).then_inc(v_plain_done, 1)

            def max_high(batch, q):
                act.wait_ge(max_turned, batch * 4 + (q + 1))
                if q:
                    act.wait_ge(max_rows_in[q - 1], batch * 32 + 32)
                else:
                    if counts(batch * 32):
                        act.wait_ge(max_rows_in[QUADS - 1], batch * 32)
                nc.scalar.copy(max_rows[:, 0, :], bank_of[f"max{q}"][0:4 * PIECES, 0:P]).then_inc(max_hi_done, 1)

            def x_turn(batch, t):
                act.wait_ge(x_turned, batch * 2 + (t + 1))
                if counts(batch * 2):
                    act.wait_ge(y_ready, batch * 2)
                nc.scalar.copy(xn2_t_parts[0][:, t, :, :].rearrange("p d r -> p (d r)"),
                               bank_of[f"x_turn{t}"][:, :]).then_inc(xn2_t_hi_done, 1)

            def hidden_turn(batch, t):
                act.wait_ge(hidden_turned, batch * 2 + (t + 1))
                act.wait_ge(hidden_ready, batch * 2 + 2)
                nc.scalar.copy(hidden_t_parts[0][:, t, :, :].rearrange("p d r -> p (d r)"),
                               bank_of[f"hidden_turn{t}"][:, :]).then_inc(hidden_t_hi_done, 1)

            def ctx_high(batch, c):
                act.wait_ge(ctx_in_sem, batch * 16 + 16)
                if counts(batch * 2):
                    act.wait_ge(v_ready, batch * 2)
                nc.scalar.copy(ctx_parts[0][:, c, :], ctx_raw[:, c, :]).then_inc(ctx_hi_done, 1)

            def xn_high(batch, c):
                act.wait_ge(xn_done, batch * 2 + (c + 1))
                if counts(batch * 4 - 1):
                    act.wait_ge(qk_ready, batch * 4 - 1)
                nc.scalar.copy(xn_parts[0][:, c, :], xn[:, c, :]).then_inc(xn_hi_done, 1)

            def split_weights(splits):
                for (hi, _), raw in splits:
                    nc.scalar.copy(hi[:, :, :], raw).then_inc(weights_hi_done, 1)

            def logits_out(batch):
                act.wait_ge(logits_ready, batch + 1)
                if counts(batch):
                    act.wait_ge(logit_turned, batch)
                nc.scalar.activation(logits_t[:, :], bank_of["logits"][0:E, 0:CH * P], ACT.Identity,
                                     bias=br_sb[:, 0:1]).then_inc(logits_t_done, 1)

            def logit_exp(batch):
                act.wait_ge(route_done, batch * ROUTE + 3)
                nc.scalar.activation(exp_logit[:, :, :], below_top[:, :, :], ACT.Exp).then_inc(exp_logit_done, 1)

            def iteration(it):
                b = it.b
                if not it.looped and b == 0:
                    act.wait_ge(later_weights_in, 16 * len(later_loads))
                    split_weights(later_splits)
                for s in range(STEPS):
                    for i in range(5):
                        if it.live(-2):
                            if (s, i) in ((0, 4), (1, 4)):
                                hidden_turn(b - 2, s)
                        if it.live(-1):
                            if (s, i) == (1, 2):
                                max_high(b - 1, 3)
                            if s in (12, 13) and i == 4:
                                x_turn(b - 1, s - 12)
                            if (s, i) == (14, 4):
                                logits_out(b - 1)
                            if (s, i) == (15, 4):
                                logit_exp(b - 1)
                        if it.live(0):
                            if (s, i) in ((5, 2), (9, 2), (12, 2)):
                                max_high(b, (s - 5 + (s == 12)) // 4)
                        if it.live(1):
                            if it.live(0) and (s, i) in ((0, 2), (2, 1)):
                                ctx_high(b + 1, s // 2)
                            if it.live(0) and (s, i) in ((3, 1), (4, 1)):
                                xn_high(b + 1, s - 3)
                            if (s, i) == (6, 3):
                                high_part(b + 1, "q0", q_hi, bq_sb, 0, 0)
                            if (s, i) == (7, 3):
                                high_part(b + 1, "k0", k_hi, bk_sb, 0, 1)
                            if (s, i) == (9, 1):
                                v_out(b + 1, 0)
                            if (s, i) == (9, 3):
                                high_part(b + 1, "q1", q_hi, bq_sb, 1, 2)
                            if (s, i) == (12, 3):
                                high_part(b + 1, "k1", k_hi, bk_sb, 1, 3)
                            if (s, i) == (13, 3):
                                v_out(b + 1, 1)
                        if not it.looped and b == 0 and (s, i) == (LAG, 0):
                            act.wait_ge(weights_lo_done, len(first_splits) + len(later_splits))
                        if i < 4 and s < LAG and it.live(-1):
                            exps(b - 1, s + LAG, i)
                        if i < 4 and s >= LAG and it.live(0):
                            exps(b, s - LAG, i)

            act.wait_ge(first_weights_in, 16 * len(first_loads))
            split_weights(first_splits[:1])
            for c in range(CH):
                xn_high(0, c)
            split_weights(first_splits[1:2])
            for c in range(CH):
                ctx_high(0, c)
            split_weights(first_splits[2:])
            run_iterations(act, iteration)

        @block.vector
        def _(dve):
            def set_zeros(to):
                nc.vector.memset(to[0:SPLIT_ROWS, 0:4, :].bitcast(F32), 0.0).then_inc(first_zeros_set, 1)

            def row_max(batch, q, piece, i):
                dve.wait_ge(s1_ready, batch * UNITS + (16 * q + 4 * piece + i + 1))
                nc.vector.tensor_reduce(neg_max[:, q, i, piece:piece + 1], s1_bank[i % 2][:, :], X_AXIS, ALU.max,
                                        negate=True).then_inc(max_done, 1)

            def max_low(batch, q):
                dve.wait_ge(max_hi_done, batch * 4 + (q + 1))
                nc.vector.tensor_tensor(max_rows[:, 1, :], bank_of[f"max{q}"][0:4 * PIECES, 0:P], max_rows[:, 0, :],
                                        ALU.subtract).then_inc(max_lo_done, 1)

            def low_part(batch, name, hi, lo, bias, chunk, n):
                dve.wait_ge(qk_hi_done, batch * 4 + (n + 1))
                nc.vector.scalar_tensor_tensor(
                    out=lo[:, chunk, :], in0=bank_of[name][:, :], scalar=bias[:, chunk:chunk + 1],
                    in1=hi[:, chunk, :], op0=ALU.add, op1=ALU.subtract).then_inc(qk_lo_done, 1)

            def turn_quad(batch, q):
                first = batch * NORM + QUAD_NORM[q]
                if counts(first):
                    dve.wait_ge(norm_done, first)
                dve.wait_ge(pv_done, batch * STEPS + (4 * q + 4))
                nc.vector.transpose(turned[:, :, :].rearrange("p n k -> p (n k)"),
                                    pv_bank[:, :]).then_inc(norm_done, 1)

            def normalise(batch, q):
                first = batch * NORM + QUAD_NORM[q]
                dve.wait_ge(norm_done, first + 1)
                nc.vector.reciprocal(inv_sum[:, :, :], turned[:, :, KC:KC + 1]).then_inc(norm_done, 1)
                dve.wait_ge(norm_done, first + 2)
                half = slice(KC * (q % 2), KC * (q % 2) + KC)
                nc.vector.tensor_tensor(normed[:, :, half], turned[:, :, 0:KC],
                                        inv_sum[:, :, :].to_broadcast([P, BLOCKS, KC]),
                                        ALU.mult).then_inc(norm_done, 1)

            def turn_back(batch, q):
                dve.wait_ge(norm_done, batch * NORM + (QUAD_NORM[q] + 3))
                if counts(batch * 2):
                    dve.wait_ge(out_ready, batch * 2)
                nc.vector.transpose(heads_out[:, q // 2, :],
                                    normed[:, :, :].rearrange("p n k -> p (n k)")).then_inc(norm_done, 1)

            def low_rest(raw, parts, c, need_sem, need, done):
                dve.wait_ge(need_sem, need)
                nc.vector.tensor_tensor(parts[1][:, c, :], raw[:, c, :], parts[0][:, c, :],
                                        ALU.subtract).then_inc(done, 1)

            def turned_low(parts, name, t, need_sem, need, done):
                dve.wait_ge(need_sem, need)
                hi, lo = (part[:, t, :, :].rearrange("p d r -> p (d r)") for part in parts)
                nc.vector.tensor_tensor(lo, bank_of[f"{name}{t}"][:, :], hi, ALU.subtract).then_inc(done, 1)

            def statistics(c, source, stats, done):
                nc.vector.bn_stats(stats[:, c, :], source[:, c, :]).then_inc(done, 1)

            def mean_variance(batch, c, stats, mean_var, done):
                dve.wait_ge(done, batch * 4 + (2 * c + 1))
                stand_alone(dve, passed)
                nc.vector.bn_aggr(mean_var[:, c, :], stats[:, c, :]).then_inc(done, 1)

            def scale_rows(c, to, source, mean_var, rstd, done):
                nc.vector.tensor_scalar(to[:, c, :], source[:, c, :], mean_var[:, c, 0:1], rstd[:, c:c + 1],
                                        ALU.subtract, ALU.mult).then_inc(done, 1)

            def statistics1(batch, c):
                dve.wait_ge(x_in, batch * 16 + 16)
                statistics(c, xn, stats1, stats1_done)

            def layernorm1(batch, c):
                dve.wait_ge(rstd1_done, batch + 1)
                scale_rows(c, xn, xn, mean_var1, rstd1, xn_done)

            def residual(batch, c):
                dve.wait_ge(out_ready, batch * 2 + (c + 1))
                dve.wait_ge(x_again_in, batch * 16 + 16)
                nc.vector.scalar_tensor_tensor(
                    out=x2[:, c, :], in0=bank_of[f"out{c}"][:, :], scalar=bo_sb[:, c:c + 1],
                    in1=x2[:, c, :], op0=ALU.add, op1=ALU.add).then_inc(x2_done, 1)

            def statistics2(batch, c):
                dve.wait_ge(x2_done, batch * 2 + (c + 1))
                statistics(c, x2, stats2, stats2_done)

            def layernorm2(batch, c):
                dve.wait_ge(rstd2_done, batch * 2 + (c + 1))
                if counts(batch * 16):
                    dve.wait_ge(out_stored[c], batch * 16)
                scale_rows(c, xn2, x2, mean_var2, rstd2, xn2_done)

            def route_start(batch):
                n = batch * ROUTE
                wide = [P, CH, E]
                dve.wait_ge(logit_turned, batch + 1)
                nc.vector.tensor_copy(logit[:, :, :],
                                      bank_of["logit_turn"][:, 0:CH * E].rearrange("p (t e) -> p t e", t=CH)
                                      ).then_inc(route_done, 1)
                dve.wait_ge(route_done, n + 1)
                nc.vector.tensor_reduce(top[:, :, :], logit[:, :, :], X_AXIS, ALU.max).then_inc(route_done, 1)
                dve.wait_ge(route_done, n + 2)
                nc.vector.tensor_tensor(below_top[:, :, :], logit[:, :, :], top[:, :, :].to_broadcast(wide),
                                        ALU.subtract).then_inc(route_done, 1)
                nc.vector.tensor_tensor(is_top[:, :, :], logit[:, :, :], top[:, :, :].to_broadcast(wide),
                                        ALU.is_equal).then_inc(route_done, 1)

            def route_choice(batch):
                n = batch * ROUTE
                wide = [P, CH, E]
                dve.wait_ge(route_done, n + 4)
                nc.vector.tensor_tensor(top_rank[:, :, :], is_top[:, :, :], rank[:, :, :],
                                        ALU.mult).then_inc(route_done, 1)
                dve.wait_ge(route_done, n + 5)
                nc.vector.tensor_reduce(best_rank[:, :, :], top_rank[:, :, :], X_AXIS,
                                        ALU.max).then_inc(route_done, 1)
                dve.wait_ge(route_done, n + 6)
                nc.vector.tensor_tensor(chosen[:, :, :], top_rank[:, :, :], best_rank[:, :, :].to_broadcast(wide),
                                        ALU.is_equal).then_inc(route_done, 1)

            def route_gate(batch):
                n = batch * ROUTE
                wide = [P, CH, E]
                dve.wait_ge(exp_logit_done, batch + 1)
                nc.vector.tensor_reduce(exp_sum[:, :, :], exp_logit[:, :, :], X_AXIS,
                                        ALU.add).then_inc(route_done, 1)
                dve.wait_ge(route_done, n + 8)
                nc.vector.reciprocal(weight[:, :, :], exp_sum[:, :, :]).then_inc(route_done, 1)
                dve.wait_ge(route_done, n + 9)
                nc.vector.scalar_tensor_tensor(
                    out=gate[:, :, :], in0=chosen[:, :, :], scalar=1.0 / R, in1=weight[:, :, :].to_broadcast(wide),
                    op0=ALU.mult, op1=ALU.mult).then_inc(route_done, 1)

            def gate_hidden(batch, t):
                dve.wait_ge(route_done, batch * ROUTE + ROUTE)
                dve.wait_ge(hidden_ready, batch * 2 + (t + 1))
                nc.vector.tensor_tensor(
                    hidden[:, t, :].rearrange("p (e r) -> p e r", e=E),
                    bank_of[f"hidden{t}"][:, :].rearrange("p (e r) -> p e r", e=E),
                    gate[:, t, :].unsqueeze(2).to_broadcast([P, E, R]), ALU.mult).then_inc(hidden_done, 1)

            def result(batch, t):
                dve.wait_ge(y_ready, batch * 2 + (t + 1))
                nc.vector.tensor_tensor(y_out[:, t, :], bank_of[f"y{t}"][:, :], x2[:, t, :],
                                        ALU.add).then_inc(y_done, 1)

            def iteration(it):
                b = it.b
                if not it.looped and b == 0:
                    dve.wait_ge(later_weights_in, 16 * len(later_loads))
                for s in range(STEPS):
                    for i in range(4):
                        if it.live(0):
                            row_max(b, s // PIECES, s % PIECES, i)
                        if it.live(-2):
                            if (s, i) == (0, 0):
                                route_gate(b - 2)
                            if (s, i) == (0, 1):
                                gate_hidden(b - 2, 0)
                            if (s, i) == (0, 3):
                                gate_hidden(b - 2, 1)
                            if (s, i) in ((1, 1), (3, 0)):
                                turned_low(hidden_t_parts, "hidden_turn", s // 2, hidden_t_hi_done,
                                           b * 2 + (s // 2 - 3), hidden_t_lo_done)
                            if (s, i) in ((4, 0), (6, 0)):
                                result(b - 2, s // 2 - 2)
                        if it.live(-1):
                            if (s, i) in ((1, 0), (4, 3), (8, 3)):
                                turn_quad(b - 1, s // 4 + 1)
                            if (s, i) in ((2, 0), (5, 0), (9, 0)):
                                normalise(b - 1, 1 if s == 2 else s // 4 + 1)
                            if (s, i) == (1, 3):
                                max_low(b - 1, 3)
                            if (s, i) in ((2, 2), (9, 1)):
                                turn_back(b - 1, 1 if s == 2 else 3)
                            if (s, i) in ((11, 1), (12, 0)):
                                mean_variance(b - 1, s - 11, stats2, mean_var2, stats2_done)
                            if (s, i) in ((10, 2), (11, 1)):
                                residual(b - 1, s - 10)
                            if (s, i) in ((11, 0), (11, 3)):
                                statistics2(b - 1, i // 3)
                            if (s, i) in ((12, 1), (13, 0)):
                                layernorm2(b - 1, s - 12)
                            if (s, i) in ((13, 1), (14, 1)):
                                turned_low(xn2_t_parts, "x_turn", s - 13, xn2_t_hi_done, b * 2 + (s - 14),
                                           xn2_t_lo_done)
                            if (s, i) == (15, 2):
                                route_start(b - 1)
                            if (s, i) == (15, 3):
                                route_choice(b - 1)
                        if it.live(0):
                            if (s, i) in ((5, 3), (9, 2), (12, 2)):
                                max_low(b, (s - 5 + (s == 12)) // 4)
                            if (s, i) == (12, 3):
                                turn_quad(b, 0)
                            if (s, i) == (14, 0):
                                normalise(b, 0)
                        if it.live(1) and it.live(0):
                            if (s, i) in ((2, 3), (3, 2)):
                                layernorm1(b + 1, s - 2)
                        if it.live(2):
                            if (s, i) in ((14, 3), (15, 1)):
                                mean_variance(b + 2, s - 14, stats1, mean_var1, stats1_done)
                            if (s, i) in ((14, 2), (15, 0)):
                                statistics1(b + 2, s - 14)
                        if it.live(1):
                            if (s, i) == (7, 0):
                                low_part(b + 1, "q0", q_hi, q_lo, bq_sb, 0, 0)
                            if (s, i) == (8, 0):
                                low_part(b + 1, "k0", k_hi, k_lo, bk_sb, 0, 1)
                            if (s, i) == (10, 0):
                                low_part(b + 1, "q1", q_hi, q_lo, bq_sb, 1, 2)
                            if (s, i) == (13, 2):
                                low_part(b + 1, "k1", k_hi, k_lo, bk_sb, 1, 3)

            set_zeros(q_stack)
            for c in range(CH):
                statistics1(0, c)
                mean_variance(0, c, stats1, mean_var1, stats1_done)
            set_zeros(k_stack)
            for c in range(CH):
                layernorm1(0, c)
            for c in range(CH):
                low_rest(xn, xn_parts, c, xn_hi_done, c + 1, xn_lo_done)
            for c in range(CH):
                low_rest(ctx_raw, ctx_parts, c, ctx_hi_done, c + 1, ctx_lo_done)
            dve.wait_ge(first_weights_in, 16 * len(first_loads))
            dve.wait_ge(ident_set, 6)
            run_iterations(dve, iteration)

        @block.tensor
        def _(pe):
            def scores_for_max(batch, s, i):
                q, head, rows = s // PIECES, 4 * (s // PIECES) + i, slice(P * (s % PIECES), P * (s % PIECES) + P)
                if s % PIECES == 0 and i == 0:
                    pe.wait_ge(stack_in[q], batch * 96 + 96)
                if counts(batch * UNITS + (4 * s + i - 1)):
                    pe.wait_ge(max_done, batch * UNITS + (4 * s + i - 1))
                nc.tensor.matmul(s1_bank[i % 2][:, :], q_stack[0:SPLIT_ROWS, head, rows],
                                 k_stack[0:SPLIT_ROWS, head, :], start=True, stop=True).then_inc(s1_ready, 1)

            def scores_less_max(batch, s, i):
                q, head, rows = s // PIECES, 4 * (s // PIECES) + i, slice(P * (s % PIECES), P * (s % PIECES) + P)
                if s % PIECES == 0 and i == 0:
                    pe.wait_ge(max_rows_in[q], batch * 32 + 32)
                if counts(batch * UNITS + (4 * s + i - 1)):
                    pe.wait_ge(exp_done, batch * UNITS + (4 * s + i - 1))
                nc.tensor.matmul(s2_bank[i % 2][:, :], k_stack[0:FULL_ROWS, head, rows],
                                 q_stack[0:FULL_ROWS, head, :], start=True, stop=True).then_inc(s2_ready, 1)

            def probs_times_v(batch, s):
                q, piece = s // PIECES, s % PIECES
                if piece == 0:
                    pe.wait_ge(v_ones_done, batch * 4 + (q + 1))
                    last = QUAD_NORM[q - 1] if q else QUAD_NORM[QUADS - 1] - NORM
                    if counts(batch * NORM + (last + 1)):
                        pe.wait_ge(norm_done, batch * NORM + (last + 1))
                pe.wait_ge(exp_done, batch * UNITS + (4 * s + 4))
                for i in range(4):
                    last = nc.tensor.matmul(pv_bank[32 * i:32 * i + 32, :], v_ones[:, q, piece, (KC + 1) * i:(KC + 1) * i + 32],
                                            probs[:, s % 2, i, :], start=piece == 0, stop=piece == PIECES - 1)
                last.then_inc(pv_done, 1)

            def products(chunks):
                return [(part, other, chunk) for part, other in ((0, 0), (0, 1), (1, 0)) for chunk in range(chunks)]

            def project(name, weights, source, c, n):
                part, w_part, kc = products(CH)[n]
                return nc.tensor.matmul(bank_of[name][:, :], weights[w_part][:, kc, P * c:P * c + P],
                                        source[part][:, kc, :], start=n == 0, stop=n == len(products(CH)) - 1)

            def query(it, c, share):
                b = it.b
                if share == 0:
                    if c == 1:
                        pe.wait_ge(qk_lo_done, b * 4 + 5)
                    elif it.live(-2):
                        pe.wait_ge(y_done, b * 2 - 3)
                    elif it.live(0):
                        pe.wait_ge(qk_lo_done, b * 4 + 4)
                    pe.wait_ge(xn_hi_done, b * 2 + 4)
                    if not it.looped and b == -1:
                        pe.wait_ge(weights_lo_done, 1)
                for n in range(2 * share, 2 * share + 2):
                    if n >= 4:
                        pe.wait_ge(xn_lo_done, b * 2 + (n - 1))
                    last = project(f"q{c}", wq_parts, xn_parts, c, n)
                if share == 2:
                    last.then_inc(qk_ready, 1)

            def key(it, c, share):
                b = it.b
                if share == 0:
                    if c == 1:
                        pe.wait_ge(qk_lo_done, b * 4 + 7)
                    elif it.live(-2):
                        pe.wait_ge(y_done, b * 2 - 2)
                    elif it.live(-1):
                        pe.wait_ge(max_lo_done, b * 4)
                    elif it.live(0):
                        pe.wait_ge(qk_lo_done, b * 4 + 2)
                    pe.wait_ge(ctx_lo_done, b * 2 + 4)
                    if not it.looped and b == -1:
                        pe.wait_ge(weights_lo_done, 2)
                for n in range(2 * share, 2 * share + 2):
                    last = project(f"k{c}", wk_parts, ctx_parts, c, n)
                if share == 2:
                    last.then_inc(qk_ready, 1)

            def value(it, half, share, shares):
                b = it.b
                if share == 0:
                    if half == 0 and it.live(0):
                        pe.wait_ge(max_lo_done, b * 4 + 1)
                    elif half == 1 and it.live(0):
                        pe.wait_ge(max_lo_done, b * 4 + 3)
                    elif half == 1:
                        pe.wait_ge(v_plain_done, b * 2 + 3)
                if not it.looped and b == -1:
                    pe.wait_ge(weights_lo_done, 3)
                each = [(n, *product) for n in range(2) for product in products(CH)]
                for m in range(len(each) // shares * share, len(each) // shares * (share + 1)):
                    n, part, w_part, kc = each[m]
                    rows = slice(P * (2 * half + n), P * (2 * half + n) + P)
                    last = nc.tensor.matmul(bank_of[f"v{half}"][:, C * n:C * n + C], ctx_parts[part][:, kc, rows],
                                            wv_parts[w_part][:, kc, :], start=m % 6 == 0, stop=m % 6 == 5)
                if share == shares - 1:
                    last.then_inc(v_ready, 1)

            def output(it, c, half):
                b = it.b
                if half == 0:
                    if c == 0 and it.live(1):
                        pe.wait_ge(v_plain_done, b * 2 + 3)
                    elif c == 1 and it.live(0):
                        pe.wait_ge(max_lo_done, b * 4 + 2)
                if c == 0:
                    pe.wait_ge(norm_done, b * NORM + (0 if half else QUAD_NORM[1] + 4 - NORM))
                last = nc.tensor.matmul(bank_of[f"out{c}"][:, :], wo_sb[:, half, P * c:P * c + P],
                                        heads_out[:, half, :], start=half == 0, stop=half == CH - 1)
                if half == 1:
                    last.then_inc(out_ready, 1)

            def turn_max(it, off, q):
                b = it.b
                if q == 3 and it.live(-2):
                    pe.wait_ge(route_done, b * ROUTE + (1 - 2 * ROUTE))
                elif q == 3:
                    pe.wait_ge(max_lo_done, b * 4 - 2)
                elif q == 0 and it.live(-2):
                    pe.wait_ge(hidden_t_lo_done, b * 2 - 2)
                elif q == 0:
                    pe.wait_ge(v_plain_done, b * 2 + 2)
                elif q == 1 and it.live(1):
                    pe.wait_ge(qk_lo_done, b * 4 + 6)
                elif q == 1:
                    pe.wait_ge(y_done, b * 2 - 2)
                elif it.live(-1):
                    pe.wait_ge(x2_done, b * 2 - 1)
                else:
                    pe.wait_ge(v_plain_done, b * 2 + 3)
                pe.wait_ge(max_done, (b + off) * UNITS + (16 * q + 16))
                nc.tensor.matmul(bank_of[f"max{q}"][0:4 * PIECES, 0:P], neg_max[:, q, :, :].rearrange("p h s -> p (h s)"),
                                 ident[:, :], start=True, stop=True).then_inc(max_turned, 1)

            def turn_x(batch, t):
                if t == 0:
                    pe.wait_ge(x2_done, batch * 2 + 2)
                else:
                    pe.wait_ge(xn2_t_lo_done, batch * 2 + 1)
                pe.wait_ge(xn2_done, batch * 2 + (t + 1))
                for d in range(DCH):
                    last = nc.tensor.transpose(bank_of[f"x_turn{t}"][:, P * d:P * d + P],
                                               xn2[:, t, P * d:P * d + P], ident[:, :])
                last.then_inc(x_turned, 1)

            def router(it, half):
                if half == 0:
                    if it.live(1):
                        pe.wait_ge(qk_lo_done, it.b * 4 + 8)
                    pe.wait_ge(xn2_t_hi_done, it.b * 2)
                else:
                    pe.wait_ge(xn2_t_lo_done, it.b * 2)
                for n in range(6 * half, 6 * half + 6):
                    part, w_part, d = products(DCH)[n]
                    last = nc.tensor.matmul(bank_of["logits"][0:E, 0:CH * P], wr_parts[w_part][:, d, :],
                                            xn2_t_parts[part][:, :, d, :], start=n == 0, stop=n == 11)
                if half == 1:
                    last.then_inc(logits_ready, 1)

            def turn_logits(batch):
                pe.wait_ge(logits_t_done, batch + 1)
                stand_alone(pe, passed)
                for t in range(CH):
                    last = nc.tensor.transpose(bank_of["logit_turn"][:, E * t:E * t + E],
                                               logits_t[:, P * t:P * t + P], ident[0:E, 0:E])
                last.then_inc(logit_turned, 1)

            def expert_in(it, batch, t, unit):
                if unit == 0:
                    if t == 0 and it.live(1):
                        pe.wait_ge(v_plain_done, it.b * 2 + 4)
                    elif t == 0 and it.live(0):
                        pe.wait_ge(max_lo_done, it.b * 4 + 3)
                    pe.wait_ge(xn2_t_hi_done, batch * 2 + (t + 1))
                for n in range(3 * unit, 3 * unit + 3):
                    if n == 2 * DCH:
                        pe.wait_ge(xn2_t_lo_done, batch * 2 + (t + 1))
                    part, a_part, d = products(DCH)[n]
                    last = nc.tensor.matmul(bank_of[f"hidden{t}"][:, :], xn2_t_parts[part][:, t, d, :],
                                            a_parts[a_part][:, d, :], start=n == 0, stop=n == 11)
                if unit == 3:
                    last.then_inc(hidden_ready, 1)

            def turn_hidden(batch, t):
                if t == 1:
                    pe.wait_ge(hidden_t_lo_done, batch * 2 + 1)
                pe.wait_ge(hidden_done, batch * 2 + (t + 1))
                for d in range(DCH):
                    last = nc.tensor.transpose(bank_of[f"hidden_turn{t}"][:, P * d:P * d + P],
                                               hidden[:, t, P * d:P * d + P], ident[:, :])
                last.then_inc(hidden_turned, 1)

            def expert_out(it, batch, t, unit):
                if unit == 0:
                    if t == 0:
                        pe.wait_ge(hidden_done, batch * 2 + 2)
                    elif it.live(-1):
                        pe.wait_ge(max_lo_done, it.b * 4)
                    pe.wait_ge(hidden_t_hi_done, batch * 2 + (t + 1))
                for n in range(2 * unit, 2 * unit + 2):
                    if n == 2 * DCH:
                        pe.wait_ge(hidden_t_lo_done, batch * 2 + (t + 1))
                    part, b_part, d = products(DCH)[n]
                    last = nc.tensor.matmul(bank_of[f"y{t}"][:, :], hidden_t_parts[part][:, t, d, :],
                                            b_parts[b_part][:, d, :], start=n == 0, stop=n == 11)
                if unit == 5:
                    last.then_inc(y_ready, 1)

            def beside(it, s, i):
                b = it.b
                if it.live(-2):
                    if s == 0 and i < 3:
                        expert_in(it, b - 2, 1, i + 1)
                    if (s, i) == (0, 3):
                        turn_hidden(b - 2, 0)
                if it.live(-1) and (s, i) == (1, 0):
                    turn_max(it, -1, 3)
                if it.live(-2):
                    if (s, i) == (1, 3):
                        turn_hidden(b - 2, 1)
                    if (s, i) in FIRST_TILE_OUT:
                        expert_out(it, b - 2, 0, FIRST_TILE_OUT.index((s, i)))
                    if (s, i) in SECOND_TILE_OUT:
                        expert_out(it, b - 2, 1, SECOND_TILE_OUT.index((s, i)))
                if it.live(0) and (s, i) in TURN_MAX:
                    turn_max(it, 0, TURN_MAX.index((s, i)))
                if it.live(1):
                    if (s, i) in Q0:
                        query(it, 0, Q0.index((s, i)))
                    if (s, i) in K0:
                        key(it, 0, K0.index((s, i)))
                    if (s, i) in V0:
                        value(it, 0, V0.index((s, i)), len(V0))
                    if (s, i) in Q1:
                        query(it, 1, Q1.index((s, i)))
                if it.live(-1):
                    if (s, i) in OUTPUT:
                        n = OUTPUT.index((s, i))
                        output(it, n // 2, n % 2)
                if it.live(1):
                    if (s, i) in K1:
                        key(it, 1, K1.index((s, i)))
                    if (s, i) in V1:
                        value(it, 1, V1.index((s, i)), len(V1))
                if it.live(-1):
                    if (s, i) in ((12, 3), (13, 3)):
                        turn_x(b - 1, s - 12)
                    if s == 14 and i in (0, 2):
                        expert_in(it, b - 1, 0, i // 2)
                    if s == 14 and i in (1, 3):
                        router(it, i // 2)
                    if s == 15 and i in (0, 2):
                        expert_in(it, b - 1, 0, 2 + i // 2)
                    if (s, i) == (15, 1):
                        turn_logits(b - 1)
                    if (s, i) == (15, 3):
                        expert_in(it, b - 1, 1, 0)

            def iteration(it):
                b = it.b
                if not it.looped and b == 1:
                    pe.wait_ge(weights_lo_done, len(first_splits) + len(later_splits))
                for s in range(STEPS):
                    for i in range(4):
                        if it.live(0):
                            scores_for_max(b, s, i)
                        if s < LAG and it.live(-1):
                            scores_less_max(b - 1, s + LAG, i)
                        if s >= LAG and it.live(0):
                            scores_less_max(b, s - LAG, i)
                        if i == 2:
                            if s <= LAG and it.live(-1):
                                probs_times_v(b - 1, s + LAG - 1)
                            if s > LAG and it.live(0):
                                probs_times_v(b, s - LAG - 1)
                        beside(it, s, i)

            pe.wait_ge(first_weights_in, 16 * len(first_loads))
            pe.wait_ge(ident_set, 6)
            run_iterations(pe, iteration)


def kernel(**inputs):
    import numpy as np
    import concourse.bacc as bacc
    from concourse.bass_utils import run_bass_kernel_spmd

    a = {name: np.asarray(value) for name, value in inputs.items()}
    x, ctx = a["x"], a["ctx_2048"]

    def columns(w):
        return w.reshape(w.shape[0], -1, P).transpose(2, 1, 0)

    def by_quad(w):
        return w.reshape(QUADS, 4, KC, -1).transpose(0, 2, 1, 3).reshape(HEADS * KC, -1)

    def chunks(v):
        return v.reshape(CH, P).transpose(1, 0)

    wo = a["L0_xattn_Wo"].reshape(C, CH, 2, 4, KC).transpose(3, 2, 4, 1, 0).reshape(P, CH, C)
    expert_b = a["L0_ffn_B"].transpose(0, 2, 1).reshape(DCH, P, D).transpose(1, 0, 2)
    arrays = {
        "x": x, "ctx_in": ctx,
        "wq_t": columns(by_quad(a["L0_xattn_Wq"])), "wk_t": columns(by_quad(a["L0_xattn_Wk"])),
        "wv_t": columns(a["L0_xattn_Wv"]), "wo_t": wo,
        "bq": chunks(by_quad(a["L0_xattn_bq"])), "bk": chunks(by_quad(a["L0_xattn_bk"])),
        "bv": a["L0_xattn_bv"], "bo": chunks(a["L0_xattn_bo"]),
        "a_t": columns(a["L0_ffn_A"].reshape(E * R, D)), "b_t": expert_b,
        "wr_t": columns(a["L0_ffn_Wr"]), "br": a["L0_ffn_br"].reshape(E, 1),
    }
    arrays = {f"{name}_dram": np.ascontiguousarray(value) for name, value in arrays.items()}
    nc = bacc.Bacc("TRN2", target_bir_lowering=False, num_devices=1)
    args = [nc.dram_tensor(name, v.shape, mybir.dt.from_np(v.dtype), kind="ExternalInput").ap()
            for name, v in arrays.items()]
    args.append(nc.dram_tensor("out_dram", (BATCHES, C, T), F32, kind="ExternalOutput").ap())
    xattn_experts(nc, *args)
    r = run_bass_kernel_spmd(nc, [arrays], core_ids=[0])
    return r.results[0]["out_dram"]
```
